# Optimizing a Trainium2 kernel written in Bass

```python
import numpy as np
import jax
import jax.numpy as jnp

def _softmax(x, axis=-1):
    return jax.nn.softmax(x, axis=axis)

def _gelu(x):
    return jax.nn.gelu(x, approximate=True)

def _silu(x):
    return jax.nn.silu(x)

def _sigmoid(x):
    return jax.nn.sigmoid(x)

def _layernorm(x, axis=-1, eps=1e-05):
    m = jnp.mean(x, axis=axis, keepdims=True)
    v = jnp.var(x, axis=axis, keepdims=True)
    return (x - m) / jnp.sqrt(v + eps)

def _scatter_add(tgt, idx, src, axis=0):
    return tgt.at[idx].add(src)

def _segment_sum(src, seg, n):
    return jax.ops.segment_sum(src, seg, n)
kernel_name = 'mk_xattn_ffn_d1_seqx_r8_1b0d84'

def setup_inputs(seed: int=0):
    np.random.seed(seed)
    _w = jnp.asarray

    def _rec_inputs():
        import jax
        import jax.numpy as jnp
        _rk = jax.random.key(seed)
        x = -0.0005207 + 1.001 * jax.random.normal(jax.random.fold_in(_rk, 1), (64, 64, 256), jnp.float32)
        _lenS = 64 - jax.random.randint(jax.random.fold_in(_rk, 7), (64,), 0, max(1, 64 // 4) + 1, jnp.int32)
        _lenS2 = 64 - jax.random.randint(jax.random.fold_in(_rk, 8), (64,), 0, max(1, 64 // 4) + 1, jnp.int32)
        _ctx_2048P = jax.random.normal(jax.random.fold_in(_rk, 12), (64, 16, 256), jnp.float32)
        _ctx_2048c = jax.random.dirichlet(jax.random.fold_in(_rk, 512), 0.3 * jnp.ones((16,), jnp.float32), (64, 64))
        _ctx_2048t = jnp.einsum('bsk,bkd->bsd', _ctx_2048c, _ctx_2048P)
        _ctx_2048t = _ctx_2048t * jax.lax.rsqrt(jnp.mean(jnp.square(_ctx_2048t)) + 1e-12) * 0.953939
        ctx_2048 = -5.72187e-05 + 0.999849 * (_ctx_2048t + 0.3 * jax.random.normal(jax.random.fold_in(_rk, 612), (64, 64, 256), jnp.float32))
        _validS = jnp.arange(64)[None, :] < _lenS[:, None]
        _validS2 = jnp.arange(64)[None, :] < _lenS2[:, None]
        _causal = jnp.tril(jnp.ones((64, 64), dtype=bool))
        mask_BxSx4224_bf0 = jnp.logical_not(jnp.ones((64, 64, 528), dtype=bool))
        return (x, ctx_2048, mask_BxSx4224_bf0)
    x, ctx_2048, mask_BxSx4224_bf0 = _rec_inputs()

    def _L0_xattn_setup():
        import jax, jax.numpy as jnp
        import numpy as np
        import math
        DIM = 256
        B, Q_LEN, KV_LEN = (8, 128, 512)
        key = jax.random.key(seed)
        ks = jax.random.split(key, 8)
        x = jax.random.normal(ks[0], (B, Q_LEN, DIM), dtype=jnp.float32)
        mask = jnp.zeros((B, Q_LEN, KV_LEN + Q_LEN), dtype=bool)
        k_cache = jax.random.normal(ks[1], (B, KV_LEN, DIM), dtype=jnp.float32)
        v_cache = jax.random.normal(ks[2], (B, KV_LEN, DIM), dtype=jnp.float32)
        scale = 1.0 / math.sqrt(DIM)
        wq = jax.random.normal(ks[3], (DIM, DIM), dtype=jnp.float32) * scale
        wk = jax.random.normal(ks[4], (DIM, DIM), dtype=jnp.float32) * scale
        wv = jax.random.normal(ks[5], (DIM, DIM), dtype=jnp.float32) * scale
        wo = jax.random.normal(ks[6], (DIM, DIM), dtype=jnp.float32) * scale
        return {'x': x, 'mask': mask, 'k_cache': k_cache, 'v_cache': v_cache, 'wq': wq, 'wk': wk, 'wv': wv, 'wo': wo}
    _L0_xattn_all = _L0_xattn_setup()
    _L0_xattn_in = {k: v for k, v in _L0_xattn_all.items() if k in ('wq', 'wk', 'wv', 'wo')}
    del _L0_xattn_all

    def _L0_ffn_setup():
        import jax, jax.numpy as jnp
        import numpy as np
        B, S, H = (1, 128, 256)
        E, F, FS = (32, 96, 512)
        TOP_K = 4
        SCALE = 0.02
        key = jax.random.key(seed)
        ks = jax.random.split(key, 9)
        return {'hidden_states': jax.random.normal(ks[0], (B, S, H), jnp.float32), 'router_weight': jax.random.normal(ks[1], (E, H), jnp.float32) * SCALE, 'w_gate': jax.random.normal(ks[2], (E, H, F), jnp.float32) * SCALE, 'w_up': jax.random.normal(ks[3], (E, H, F), jnp.float32) * SCALE, 'w_down': jax.random.normal(ks[4], (E, F, H), jnp.float32) * SCALE, 'sw_gate': jax.random.normal(ks[5], (H, FS), jnp.float32) * SCALE, 'sw_up': jax.random.normal(ks[6], (H, FS), jnp.float32) * SCALE, 'sw_down': jax.random.normal(ks[7], (FS, H), jnp.float32) * SCALE, 'sgate_w': jax.random.normal(ks[8], (H, 1), jnp.float32) * SCALE}
    _L0_ffn_all = _L0_ffn_setup()
    _L0_ffn_in = {k: v for k, v in _L0_ffn_all.items() if k in ('router_weight', 'w_gate', 'w_up', 'w_down', 'sw_gate', 'sw_up', 'sw_down', 'sgate_w')}
    del _L0_ffn_all
    return {'x': x, 'ctx_2048': ctx_2048, 'mask_BxSx4224_bf0': mask_BxSx4224_bf0, 'L0_xattn_wq': _L0_xattn_in['wq'], 'L0_xattn_wk': _L0_xattn_in['wk'], 'L0_xattn_wv': _L0_xattn_in['wv'], 'L0_xattn_wo': _L0_xattn_in['wo'], 'L0_ffn_router_weight': _L0_ffn_in['router_weight'], 'L0_ffn_w_gate': _L0_ffn_in['w_gate'], 'L0_ffn_w_up': _L0_ffn_in['w_up'], 'L0_ffn_w_down': _L0_ffn_in['w_down'], 'L0_ffn_sw_gate': _L0_ffn_in['sw_gate'], 'L0_ffn_sw_up': _L0_ffn_in['sw_up'], 'L0_ffn_sw_down': _L0_ffn_in['sw_down'], 'L0_ffn_sgate_w': _L0_ffn_in['sgate_w']}

def reference(x, ctx_2048, mask_BxSx4224_bf0, L0_xattn_wq, L0_xattn_wk, L0_xattn_wv, L0_xattn_wo, L0_ffn_router_weight, L0_ffn_w_gate, L0_ffn_w_up, L0_ffn_w_down, L0_ffn_sw_gate, L0_ffn_sw_up, L0_ffn_sw_down, L0_ffn_sgate_w):
    import jax
    import jax.numpy as jnp

    def _L0_xattn_ref(x, mask, k_cache, v_cache, wq, wk, wv, wo):
        import jax, jax.numpy as jnp
        import numpy as np
        import math
        DIM = 256
        B, Q_LEN, KV_LEN = (8, 128, 512)
        q = jnp.einsum('bsd,ed->bse', x, wq)
        k_new = jnp.einsum('bsd,ed->bse', x, wk)
        v_new = jnp.einsum('bsd,ed->bse', x, wv)
        k = jnp.concatenate([k_cache, k_new], axis=1)
        v = jnp.concatenate([v_cache, v_new], axis=1)
        scale = 1.0 / math.sqrt(q.shape[-1])
        scores = jnp.einsum('bqd,bkd->bqk', q, k) * scale
        attn = jax.nn.softmax(scores, axis=-1)
        out = jnp.einsum('bqk,bkd->bqd', attn, v)
        return jnp.einsum('bqd,ed->bqe', out, wo)

    def _L0_ffn_ref(hidden_states, router_weight, w_gate, w_up, w_down, sw_gate, sw_up, sw_down, sgate_w):
        import jax, jax.numpy as jnp
        import numpy as np
        B, S, H = (1, 128, 256)
        E, F, FS = (32, 96, 512)
        TOP_K = 4
        SCALE = 0.02
        b, s, h = hidden_states.shape
        x = hidden_states.reshape(-1, h)
        T = x.shape[0]
        logits = x @ router_weight.T
        probs = jax.nn.softmax(logits.astype(jnp.float32), axis=-1)
        topv, topi = jax.lax.top_k(probs, TOP_K)
        topv = topv / jnp.sum(topv, axis=-1, keepdims=True)
        topv = topv.astype(probs.dtype)
        combine = jnp.zeros((T, E), probs.dtype).at[jnp.arange(T)[:, None], topi].add(topv)
        g = jnp.einsum('th,ehf->etf', x, w_gate)
        u = jnp.einsum('th,ehf->etf', x, w_up)
        act = jax.nn.silu(g) * u
        out = jnp.einsum('te,etf,efh->th', combine, act, w_down)
        shared = jax.nn.silu(x @ sw_gate) * (x @ sw_up) @ sw_down
        out = out + jax.nn.sigmoid(x @ sgate_w) * shared
        return out.reshape(b, s, h)
    x = x + _L0_xattn_ref(_layernorm(x, axis=-1), mask_BxSx4224_bf0, ctx_2048, ctx_2048, L0_xattn_wq, L0_xattn_wk, L0_xattn_wv, L0_xattn_wo)
    x = x + _L0_ffn_ref(_layernorm(x, axis=-1), L0_ffn_router_weight, L0_ffn_w_gate, L0_ffn_w_up, L0_ffn_w_down, L0_ffn_sw_gate, L0_ffn_sw_up, L0_ffn_sw_down, L0_ffn_sgate_w)
    return x

_drawn_inputs = setup_inputs


def setup_inputs(seed=0):
    import zlib

    import numpy as np

    out = dict(_drawn_inputs(seed))
    spreads = {}
    factors = {'L0_ffn_router_weight': 8.0,
     'L0_ffn_w_gate': 8.0,
     'L0_ffn_w_up': 8.0,
     'L0_ffn_w_down': 8.0,
     'L0_ffn_sw_gate': 4.911,
     'L0_ffn_sw_up': 4.829,
     'L0_ffn_sw_down': 4.861,
     'L0_ffn_sgate_w': 8.0}
    for name, (base, spread) in spreads.items():
        noise = np.random.default_rng([zlib.crc32(name.encode()), seed]).standard_normal(out[name].shape)
        drawn = base * np.exp(spread * noise) if base else spread * noise
        out[name] = jnp.asarray(drawn.astype(out[name].dtype))
    for name, factor in factors.items():
        out[name] = (out[name] * factor).astype(out[name].dtype)
    return out
```

```python
from contextlib import ExitStack

import numpy as np

import concourse.bass as bass
from concourse import mybir

ALU = mybir.AluOpType
ACT = mybir.ActivationFunctionType
AXIS = mybir.AxisListType
F32 = mybir.dt.float32
BF16 = mybir.dt.bfloat16
F16 = mybir.dt.float16
I32 = mybir.dt.int32
U32 = mybir.dt.uint32

P = 128
D = 256
DC = D // P
SEQ = 64
EXPERTS = 32
TOP = 4
F = 96
FS = 512
EPS = 1e-5
SCALE = 1.0 / 16.0


def build_xattn_moe(nc, x, ctx, ctx_t, wq_t, wk_t, wv_t, wo_t, router_t, w_gate_up, w_down,
                    sw_gate_up, sw_down, normed, expert_out, out):
    tokens = x.shape[0]
    tiles = tokens // P
    blocks = tiles // 2
    slot_tiles = tokens * TOP // P + EXPERTS
    pairs = slot_tiles // 2
    groups = tokens // 512
    GT = 4
    FB = FS // P
    XG = 4
    TC = tiles // 4
    assert slot_tiles % 2 == 0 and pairs % XG == 0 and blocks % 2 == 0 and blocks >= 6

    x_v = x.rearrange("(t p) d -> p t d", p=P)
    ctx_v = ctx.rearrange("(t p) d -> p t d", p=P)
    ctx_t_v = ctx_t.rearrange("(c p) t -> p c t", p=P)
    out_v = out.rearrange("(t p) d -> p t d", p=P)
    normed_v = normed.rearrange("(t p) d -> p t d", p=P)
    expert_out_v = expert_out.rearrange("(s p) d -> p s d", p=P)

    with ExitStack() as stack:
        def sb(name, shape, dt=F32):
            return stack.enter_context(nc.sbuf_tensor(name, shape, dt))

        def sem(name):
            return stack.enter_context(nc.semaphore(name))

        resid = sb("resid", [P, tiles, D])
        hnt = sb("hnt", [P, DC, tokens])
        w_gu = sb("w_gu", [P, DC, EXPERTS, 2 * F])
        ws_gu = sb("ws_gu", [P, DC, 2 * FS])
        ws_d = sb("ws_d", [P, FB, D])
        wr = sb("wr", [P, DC, EXPERTS + 1])
        ident = sb("ident", [P, P])
        arena = sb("arena", [P, 8192])
        arena2 = sb("arena2", [P, 6144])
        taken = {"arena": 0, "arena2": 0}

        def part(which, name, words):
            at = taken[name]
            taken[name] = at + words
            assert taken[name] <= which.shape[1], name
            return which[:, at:at + words]

        xn = part(arena, "arena", 2 * D).rearrange("p (j d) -> p j d", j=2)
        xnt = part(arena, "arena", DC * 256).rearrange("p (c t) -> p c t", c=DC)
        ctx_sb = [part(arena, "arena", 2 * D).rearrange("p (j d) -> p j d", j=2) for _ in range(2)]
        ctxt_sb = [part(arena, "arena", DC * 256).rearrange("p (c t) -> p c t", c=DC) for _ in range(2)]
        qt = part(arena, "arena", DC * 256).rearrange("p (c t) -> p c t", c=DC)
        kt = part(arena, "arena", DC * 256).rearrange("p (c t) -> p c t", c=DC)
        v_sb = [part(arena, "arena", 2 * D).rearrange("p (j d) -> p j d", j=2) for _ in range(2)]
        probs = part(arena, "arena", 512).rearrange("p (j s k) -> p j s k", j=2, s=2)
        probst = part(arena, "arena", 512).rearrange("p (j s q) -> p j s q", j=2, s=2)
        ot = part(arena, "arena", DC * 256).rearrange("p (c t) -> p c t", c=DC)
        hn = [part(arena, "arena", 2 * D).rearrange("p (j d) -> p j d", j=2) for _ in range(2)]

        hnt_now = part(arena, "arena", DC * 256).rearrange("p (c t) -> p c t", c=DC)

        w_dn = arena[0:F, 0:EXPERTS * D].rearrange("f (e d) -> f e d", e=EXPERTS)

        taken["arena"] = 0
        act_t = part(arena, "arena", FB * 512).rearrange("p (f t) -> p f t", f=FB)
        silu_s = [part(arena, "arena", 512) for _ in range(2)]
        picked = [part(arena, "arena", TOP * D).rearrange("p (k d) -> p k d", k=TOP) for _ in range(4)]

        w_att = [part(arena2, "arena2", DC * D).rearrange("p (c e) -> p c e", c=DC) for _ in range(4)]
        wq, wk, wv, wo = w_att
        onehot = part(arena2, "arena2", tiles * TOP * EXPERTS // 2).bitcast(BF16) \
            .rearrange("p (t k e) -> p t k e", t=tiles, k=TOP)
        posoff = part(arena2, "arena2", EXPERTS * tiles).rearrange("p (e t) -> p e t", e=EXPERTS)
        slot_prod = part(arena2, "arena2", TC * TOP * EXPERTS) \
            .rearrange("p (t k e) -> p t k e", t=TC, k=TOP)

        taken["arena2"] = 0
        gathered = [part(arena2, "arena2", 2 * D).rearrange("p (s d) -> p s d", s=2) for _ in range(XG)]
        gt = part(arena2, "arena2", 2 * DC * P).rearrange("p (s c q) -> p s c q", s=2, c=DC)
        gate_e = part(arena2, "arena2", 2 * F).rearrange("p (s f) -> p s f", s=2)
        act_e = part(arena2, "arena2", 2 * F).rearrange("p (s f) -> p s f", s=2)
        act_et = part(arena2, "arena2", 2 * P)[0:F, :].rearrange("p (s q) -> p s q", s=2)
        down_e = [part(arena2, "arena2", 2 * D).rearrange("p (s d) -> p s d", s=2) for _ in range(4)]

        stats = sb("stats", [P, 2, 6])
        moments = sb("moments", [P, 2, 2])
        var_eps = sb("var_eps", [P, 2])
        rstd = sb("rstd", [P, 2])
        h_stats = sb("h_stats", [P, 2, 6])
        h_moments = sb("h_moments", [P, 2, 2])
        h_var_eps = sb("h_var_eps", [P, 2])
        h_rstd = sb("h_rstd", [P, 2])
        neg_half = sb("neg_half", [P, 2])
        negmax = sb("negmax", [P, 2])
        rowsum = sb("rowsum", [P, 2])
        rinv = sb("rinv", [P, 2])
        logits = sb("logits", [P, 2, EXPERTS + 1])
        gate_logit = sb("gate_logit", [P, tiles])
        gate_den = sb("gate_den", [P, tiles])
        shared_gate = sb("shared_gate", [P, tiles])
        top_val = sb("top_val", [P, tiles, 8])
        top_now = sb("top_now", [P, 2, 8])
        top_idx = sb("top_idx", [P, 2, 8], U32)
        top_diff = sb("top_diff", [P, tiles, TOP])
        top_exp = sb("top_exp", [P, tiles, TOP])
        top_sum = sb("top_sum", [P, tiles])
        top_rsum = sb("top_rsum", [P, tiles])
        combine = sb("combine", [P, tiles, TOP])
        iota_e = sb("iota_e", [P, EXPERTS])
        iota_row = sb("iota_row", [P, P], F16)
        iota_tile = sb("iota_tile", [P, slot_tiles], F16)
        iota_start = sb("iota_start", [EXPERTS, slot_tiles])
        token_id = sb("token_id", [P, tiles])
        before = sb("before", [P, P], BF16)
        ones = sb("ones", [P, P], BF16)
        ones_h = sb("ones_h", [P, P], F16)
        upto = sb("upto", [EXPERTS, EXPERTS])
        zeros = sb("zeros", [P, slot_tiles], F16)
        chosen = sb("chosen", [P, EXPERTS, tiles + 1], BF16)
        restart = sb("restart", [P, EXPERTS, tiles + 1], BF16)
        earlier = sb("earlier", [P, EXPERTS, tiles + 1], BF16)
        count_i = sb("count_i", [P, EXPERTS], I32)
        padded_i = sb("padded_i", [P, EXPERTS], I32)
        padded = sb("padded", [P, EXPERTS])
        ones_e = sb("ones_e", [P, EXPERTS])
        ends = sb("ends", [P, EXPERTS])
        starts = sb("starts", [P, EXPERTS])
        count_ci = sb("count_ci", [EXPERTS, 1], I32)
        padded_ci = sb("padded_ci", [EXPERTS, 1], I32)
        padded_c = sb("padded_c", [EXPERTS, 1])
        ends_c = sb("ends_c", [EXPERTS, 1])
        past = sb("past", [EXPERTS, slot_tiles], BF16)
        tile_expert = sb("tile_expert", [1, 2 + slot_tiles], I32)
        slot_f = sb("slot_f", [P, tiles, TOP])
        slot = sb("slot", [P, tiles, TOP], I32)
        slot_row_i = sb("slot_row_i", [P, tiles, TOP], I32)
        slot_tile_i = sb("slot_tile_i", [P, tiles, TOP], I32)
        slot_row = sb("slot_row", [P, tiles, TOP])
        slot_tile = sb("slot_tile", [P, tiles, TOP])
        row_hot = sb("row_hot", [P, 2, TOP, P], F16)
        tile_hot = sb("tile_hot", [P, 2, TOP, slot_tiles], F16)
        slot_token = sb("slot_token", [P, slot_tiles], I32)
        gather_idx = sb("gather_idx", [P, XG, 2], I32)
        pick_idx = sb("pick_idx", [P, 4, TOP], I32)

        psum = [stack.enter_context(nc.psum_tensor(f"bank{i}", [P, 512], F32)) for i in range(8)]
        b_t, b_q, b_k, b_v, b_s, b_p, b_o, b_y = psum

        logit_view = b_p[:, 0:2 * (EXPERTS + 1)].rearrange("p (j e) -> p j e", j=2)
        gu_view = b_q[:, 0:4 * F].rearrange("p (s f) -> p s f", s=2)
        THIRDS = [(0, 11), (11, 22), (22, EXPERTS)]

        S = {n: sem(n) for n in (
            "consts", "att_w", "shared_w", "expert_w", "down_w",
            "x_stats", "x_moments", "x_var", "x_rstd", "xn_ready", "xnt_psum", "xnt_ready",
            "q_psum", "qt_ready", "k_psum", "kt_ready", "v_psum", "v_ready",
            "scores_psum", "negmax_ready", "probs_ready", "probst_psum", "probst_ready",
            "o_psum", "ot_ready", "y_psum", "rinv_ready", "attended",
            "h_stats_s", "h_moments_s", "h_var_s", "h_rstd_s", "hn_ready", "hnt_psum", "hnt_ready", "hnt_kept",
            "logits_psum", "logits_ready", "top_val_ready", "top_idx_ready", "onehot_ready",
            "chosen_ready",
            "route_dve", "route_pe", "route_act", "hot_ready", "hot_used", "tables_ready",
            "idx_copied", "gt_psum", "gt_ready", "gu_psum", "gate_e_ready", "act_e_ready",
            "act_et_psum", "act_et_ready", "down_psum", "down_ready",
            "sg_psum", "su_psum", "silu_ready", "shared_act", "shared_psum", "shared_added",
            "pick_copied", "pick_step", "out_done", "dve_consts", "passed_pool",
            "passed_dve")}
        x_in = [sem(f"x_in{u}") for u in range(2)]
        ctx_in = [sem(f"ctx_in{u}") for u in range(2)]
        ctxt_in = [sem(f"ctxt_in{u}") for u in range(2)]
        hn_stored = [sem(f"hn_stored{u}") for u in range(2)]
        gather_in = [sem(f"gather_in{u}") for u in range(XG)]
        down_stored = [sem(f"down_stored{u}") for u in range(4)]
        pick_in = [sem(f"pick_in{u}") for u in range(4)]

        DVE_CONSTS = 6
        MARK = {"earlier": 1, "diffs": 2, "padded_c": 7, "past": 12}
        CONSTS = 15

        def wait(eng, name, count):
            if isinstance(count, int) and count <= 0:
                return
            eng.wait_ge(S[name], count)

        def apart(eng, count, semaphore):
            if isinstance(count, int) and count <= 0:
                return
            eng.wait_ge(semaphore, count)
            if not isinstance(count, int):
                eng.sem_inc(S["passed_pool"] if eng is nc.gpsimd else S["passed_dve"], 1)

        def there(i, off):
            return not isinstance(i, int) or 0 <= 2 * i + off < blocks

        def number(i, off):
            return 2 * i + off, i + off // 2, off % 2

        def pipeline(eng, step, first=-2, last=None):
            last = blocks if last is None else last
            for n in range(first, 3):
                step(0, n)
            loops = (blocks - 3) // 2
            with eng.Fori(1, loops) as i:
                step(i, 1)
                step(i, 2)
            for n in range(2 * loops + 1, last + 1):
                step(0, n)

        block = stack.enter_context(nc.Block())

        @block.sync
        def _(sp):
            sp.dma_start(resid[:, 0:2, :], x_v[:, 0:2, :]).then_inc(x_in[0], 16)

            def load(i, off):
                if not there(i, off):
                    return
                b, n, u = number(i, off)
                if not (isinstance(b, int) and b == 0):
                    if not isinstance(n, int) or n > 0:
                        sp.wait_ge(x_in[u], 16 * n)
                    sp.dma_start(resid[:, bass.ds(2 * b, 2), :], x_v[:, bass.ds(2 * b, 2), :]) \
                        .then_inc(x_in[u], 16)
                wait(sp, "scores_psum", b - 1)
                sp.dma_start(ctxt_sb[u], ctx_t_v[:, :, bass.ds(256 * b, 256)]).then_inc(ctxt_in[u], 16)
                wait(sp, "o_psum", b - 1)
                sp.dma_start(ctx_sb[u], ctx_v[:, bass.ds(2 * b, 2), :]).then_inc(ctx_in[u], 16)

            def store_hn(i, off):
                if not there(i, off):
                    return
                b, n, u = number(i, off)
                wait(sp, "hn_ready", b + 1)
                sp.dma_start(normed_v[:, bass.ds(2 * b, 2), :], hn[u]).then_inc(hn_stored[u], 16)
                e = EXPERTS // blocks
                sp.dma_start(w_gu[:, :, bass.ds(e * b, e), :], w_gate_up[:, :, bass.ds(e * b, e), :]) \
                    .then_inc(S["expert_w"], 16)

            def step(i, off):
                load(i, off + 2)
                store_hn(i, off)

            pipeline(sp, step)
            sp.dma_start(ws_gu[:, :, :], sw_gate_up).then_inc(S["shared_w"], 16)
            sp.dma_start(ws_d[:, :, :], sw_down).then_inc(S["shared_w"], 16)
            sp.wait_ge(S["logits_ready"], blocks)
            sp.wait_ge(S["hnt_kept"], blocks)
            for u in range(2):
                sp.wait_ge(hn_stored[u], 16 * (blocks // 2))
            sp.dma_start(w_dn, w_down).then_inc(S["down_w"], 16)

            with sp.Fori(0, pairs // 4) as i:
                for u in range(4):
                    sp.wait_ge(S["down_ready"], 4 * i + (u + 1))
                    sp.dma_start(expert_out_v[:, bass.ds(8 * i + 2 * u, 2), :], down_e[u]) \
                        .then_inc(down_stored[u], 16)

            with sp.Fori(0, groups) as g:
                sp.wait_ge(S["shared_added"], GT * g + GT)
                sp.dma_start(out_v[:, bass.ds(GT * g, GT), :], resid[:, bass.ds(GT * g, GT), :]) \
                    .then_inc(S["out_done"], 16)
            sp.wait_ge(S["out_done"], 16 * groups)

        @block.gpsimd
        def _(pool):
            c = S["consts"]

            pool.memset(ident[:, :], 0.0).then_inc(c, 1)
            pool.memset(before[:, :], 1.0).then_inc(c, 1)
            pool.memset(upto[:, :], 1.0).then_inc(c, 1)
            pool.wait_ge(c, 3)
            pool.affine_select(out=ident[:, :], in_=ident[:, :], compare_op=ALU.not_equal, fill=1.0,
                               base=0, pattern=[[-1, P]], channel_multiplier=1).then_inc(c, 1)
            pool.affine_select(out=before[:, :], in_=before[:, :], compare_op=ALU.is_ge, fill=0.0,
                               base=-1, pattern=[[1, P]], channel_multiplier=-1).then_inc(c, 1)
            pool.affine_select(out=upto[:, :], in_=upto[:, :], compare_op=ALU.is_ge, fill=0.0,
                               base=0, pattern=[[1, EXPERTS]], channel_multiplier=-1).then_inc(c, 1)
            pool.memset(neg_half[:, :], -0.5).then_inc(c, 1)
            pool.iota(iota_e[:, :], [[1, EXPERTS]], base=0, channel_multiplier=0,
                      allow_small_or_imprecise_dtypes=True).then_inc(c, 1)
            pool.iota(iota_row[:, :], [[1, P]], base=0, channel_multiplier=0,
                      allow_small_or_imprecise_dtypes=True).then_inc(c, 1)
            pool.iota(iota_tile[:, :], [[1, slot_tiles]], base=0, channel_multiplier=0,
                      allow_small_or_imprecise_dtypes=True).then_inc(c, 1)
            pool.iota(iota_start[:, :], [[P, slot_tiles]], base=0, channel_multiplier=0,
                      allow_small_or_imprecise_dtypes=True).then_inc(c, 1)
            pool.iota(token_id[:, :], [[P, tiles]], base=-tokens // 2, channel_multiplier=1,
                      allow_small_or_imprecise_dtypes=True).then_inc(c, 1)
            pool.memset(zeros[:, :], 0.0).then_inc(c, 1)
            pool.memset(ones[:, :], 1.0).then_inc(c, 1)
            pool.memset(ones_e[:, :], 1.0).then_inc(c, 1)
            pool.wait_ge(c, CONSTS)

            def inverse_root(n, moments_sem, moms, veps, var_sem, out_r, rstd_sem):
                apart(pool, n + 1, S[moments_sem])
                pool.tensor_scalar(veps[:, :], moms[:, :, 1], EPS, None, ALU.add).then_inc(S[var_sem], 1)
                pool.wait_ge(S[var_sem], n + 1)
                pool.tensor_tensor(out_r[:, :], veps[:, :], neg_half[:, :], ALU.pow) \
                    .then_inc(S[rstd_sem], 1)

            def step(i, off):
                if there(i, off + 2):
                    inverse_root(number(i, off + 2)[0], "x_moments", moments, var_eps, "x_var", rstd,
                                 "x_rstd")
                if there(i, off):
                    inverse_root(number(i, off)[0], "h_moments_s", h_moments, h_var_eps, "h_var_s",
                                 h_rstd, "h_rstd_s")
                if there(i, off - 1):
                    b = number(i, off - 1)[0]
                    apart(pool, b + 1, S["hnt_ready"])
                    pool.tensor_copy(hnt[:, :, bass.ds(256 * b, 256)], hnt_now) \
                        .then_inc(S["hnt_kept"], 1)

            pipeline(pool, step)

            pool.wait_ge(S["tables_ready"], 2)
            for u in range(2):
                pool.wait_ge(hn_stored[u], 16 * (blocks // 2))

            def gather(i, u):
                pair = XG * i + u
                apart(pool, 32 * i, gather_in[u])
                pool.tensor_copy(gather_idx[:, u, :], slot_token[:, bass.ds(2 * pair, 2)]) \
                    .then_inc(S["idx_copied"], 1)
                apart(pool, pair - (XG - 1), S["gt_psum"])
                apart(pool, pair + 1, S["idx_copied"])
                for s in range(2):
                    pool.indirect_dma_start(
                        out=gathered[u][:, s, :], out_offset=None, in_=normed,
                        in_offset=bass.IndirectOffsetOnAxis(ap=gather_idx[:, u, s:s + 1], axis=0),
                    ).then_inc(gather_in[u], 16)

            for u in range(XG):
                gather(0, u)
            with pool.Fori(1, pairs // XG) as i:
                for u in range(XG):
                    gather(i, u)

            for u in range(4):
                pool.wait_ge(down_stored[u], 16 * (pairs // 4))
            pool.wait_ge(S["down_psum"], pairs)

            def pick(i, u):
                t = 4 * i + u
                apart(pool, 64 * i, pick_in[u])
                pool.tensor_copy(pick_idx[:, u, :], slot[:, bass.ds(t, 1), :]
                                 .rearrange("p t k -> p (t k)")).then_inc(S["pick_copied"], 1)
                apart(pool, TOP * (t - 3), S["pick_step"])
                apart(pool, t + 1, S["pick_copied"])
                for k in range(TOP):
                    pool.indirect_dma_start(
                        out=picked[u][:, k, :], out_offset=None, in_=expert_out,
                        in_offset=bass.IndirectOffsetOnAxis(ap=pick_idx[:, u, k:k + 1], axis=0),
                    ).then_inc(pick_in[u], 16)

            for u in range(4):
                pick(0, u)
            with pool.Fori(1, tiles // 4) as i:
                for u in range(4):
                    pick(i, u)

        @block.scalar
        def _(act):
            for w, src in zip(w_att, (wq_t, wk_t, wv_t, wo_t)):
                act.dma_start(w, src.rearrange("(c p) e -> p c e", p=P)).then_inc(S["att_w"], 16)
            act.dma_start(wr[:, :, :], router_t.rearrange("(c p) e -> p c e", p=P)) \
                .then_inc(S["att_w"], 16)
            act.wait_ge(S["dve_consts"], DVE_CONSTS)

            def step(i, off):
                if there(i, off + 1):
                    b = number(i, off + 1)[0]
                    wait(act, "v_psum", b)
                    wait(act, "xnt_psum", b + 1)
                    act.copy(xnt.rearrange("p c t -> p (c t)"), b_t[:, :]).then_inc(S["xnt_ready"], 1)
                if there(i, off):
                    b = number(i, off)[0]
                    scores = b_s[:, :].rearrange("p (j s k) -> p j s k", j=2, s=2)
                    wait(act, "negmax_ready", b + 1)
                    for h in range(2):
                        rows = slice(SEQ * h, SEQ * h + SEQ)
                        for j in range(2):
                            last = act.activation(probs[rows, j, :, rows], scores[rows, j, :, rows],
                                                  ACT.Exp, bias=negmax[rows, j:j + 1],
                                                  accum_out=rowsum[rows, j:j + 1])
                    last.then_inc(S["probs_ready"], 1)
                    wait(act, "probst_psum", b + 1)
                    act.copy(probst.rearrange("p j s q -> p (j s q)"), b_p[:, :]) \
                        .then_inc(S["probst_ready"], 1)
                    wait(act, "y_psum", b)
                    wait(act, "o_psum", b + 1)
                    act.copy(ot.rearrange("p c t -> p (c t)"), b_o[:, :]).then_inc(S["ot_ready"], 1)
                if there(i, off - 1):
                    b = number(i, off - 1)[0]
                    wait(act, "logits_psum", b)
                    wait(act, "hnt_kept", b)
                    wait(act, "hnt_psum", b + 1)
                    act.copy(hnt_now.rearrange("p c t -> p (c t)"), b_t[:, :]) \
                        .then_inc(S["hnt_ready"], 1)

            pipeline(act, step)

            act.wait_ge(S["route_dve"], MARK["diffs"])
            act.activation(top_exp[:, :, :], top_diff[:, :, :], ACT.Exp).then_inc(S["route_act"], 1)
            act.activation(gate_den[:, :], gate_logit[:, :], ACT.Exp, scale=-1.0) \
                .then_inc(S["route_act"], 1)

            act.wait_ge(S["tables_ready"], 2)

            def expert_gt(pair):
                wait(act, "gu_psum", pair)
                wait(act, "gt_psum", pair + 1)
                act.copy(gt.rearrange("p s c q -> p (s c q)"), b_t[:, :]).then_inc(S["gt_ready"], 1)

            def expert_silu(pair):
                wait(act, "act_e_ready", pair)
                wait(act, "gu_psum", pair + 1)
                act.activation(gate_e, gu_view[:, :, 0:F], ACT.Silu).then_inc(S["gate_e_ready"], 1)

            expert_gt(0)
            expert_silu(0)
            with act.Fori(1, pairs) as p:
                expert_gt(p)
                expert_silu(p)

            def shared_silu(i, u):
                n = FB * i + u
                wait(act, "shared_act", n - 1)
                wait(act, "sg_psum", n + 1)
                act.activation(silu_s[u % 2], (b_t, b_q)[u % 2][:, :], ACT.Silu) \
                    .then_inc(S["silu_ready"], 1)

            for u in range(FB):
                shared_silu(0, u)
            with act.Fori(1, groups) as g:
                for u in range(FB):
                    shared_silu(g, u)

        @block.tensor
        def _(pe):
            pe.wait_ge(S["consts"], CONSTS)
            pe.wait_ge(S["att_w"], 16 * 5)
            pe.wait_ge(S["dve_consts"], DVE_CONSTS)

            def step(i, off):
                if there(i, off + 1):
                    b = number(i, off + 1)[0]
                    wait(pe, "xn_ready", b + 1)
                    for c in range(DC):
                        for j in range(2):
                            last = pe.transpose(b_t[:, 256 * c + P * j:256 * c + P * j + P],
                                                xn[:, j, P * c:P * c + P], ident[:, :])
                    last.then_inc(S["xnt_psum"], 1)
                if there(i, off):
                    b, n, u = number(i, off)
                    wait(pe, "qt_ready", b + 1)
                    wait(pe, "kt_ready", b + 1)
                    pe.wait_ge(ctxt_in[u], 16 * (n + 1))
                    for j in range(2):
                        for s, keys in enumerate((ctxt_sb[u], kt)):
                            at = 256 * j + P * s
                            for c in range(DC):
                                last = pe.matmul(b_s[:, at:at + P], qt[:, c, P * j:P * j + P],
                                                 keys[:, c, P * j:P * j + P],
                                                 start=(c == 0), stop=(c == DC - 1))
                    last.then_inc(S["scores_psum"], 1)
                if there(i, off + 1):
                    b = number(i, off + 1)[0]
                    wait(pe, "xnt_ready", b + 1)
                    for w, bank, name in ((wq, b_q, "q_psum"), (wk, b_k, "k_psum")):
                        for m in range(DC):
                            for c in range(DC):
                                last = pe.matmul(bank[:, 256 * m:256 * m + 256],
                                                 w[:, c, P * m:P * m + P], xnt[:, c, :],
                                                 start=(c == 0), stop=(c == DC - 1))
                        last.then_inc(S[name], 1)
                if there(i, off):
                    b = number(i, off)[0]
                    wait(pe, "logits_ready", b - 1)
                    wait(pe, "probs_ready", b + 1)
                    for j in range(2):
                        for s in range(2):
                            at = 256 * j + P * s
                            last = pe.transpose(b_p[:, at:at + P], probs[:, j, s, :], ident[:, :])
                    last.then_inc(S["probst_psum"], 1)
                if there(i, off + 1):
                    b = number(i, off + 1)[0]
                    wait(pe, "v_ready", b)
                    for j in range(2):
                        for c in range(DC):
                            last = pe.matmul(b_v[:, 256 * j:256 * j + 256],
                                             xnt[:, c, P * j:P * j + P], wv[:, c, :],
                                             start=(c == 0), stop=(c == DC - 1))
                    last.then_inc(S["v_psum"], 1)
                if there(i, off):
                    b, n, u = number(i, off)
                    wait(pe, "probst_ready", b + 1)
                    wait(pe, "v_ready", b + 1)
                    pe.wait_ge(ctx_in[u], 16 * (n + 1))
                    for c in range(DC):
                        for j in range(2):
                            at = 256 * c + P * j
                            for s, values in enumerate((ctx_sb[u], v_sb[u])):
                                last = pe.matmul(b_o[:, at:at + P], values[:, j, P * c:P * c + P],
                                                 probst[:, j, s, :], start=(s == 0), stop=(s == 1))
                    last.then_inc(S["o_psum"], 1)
                if there(i, off - 1):
                    b = number(i, off - 1)[0]
                    wait(pe, "hn_ready", b + 1)
                    for c in range(DC):
                        for j in range(2):
                            last = pe.transpose(b_t[:, 256 * c + P * j:256 * c + P * j + P],
                                                hn[number(i, off - 1)[2]][:, j, P * c:P * c + P],
                                                ident[:, :])
                    last.then_inc(S["hnt_psum"], 1)
                if there(i, off):
                    b = number(i, off)[0]
                    wait(pe, "attended", b)
                    wait(pe, "ot_ready", b + 1)
                    for j in range(2):
                        for c in range(DC):
                            last = pe.matmul(b_y[:, 256 * j:256 * j + 256],
                                             ot[:, c, P * j:P * j + P], wo[:, c, :],
                                             start=(c == 0), stop=(c == DC - 1))
                    last.then_inc(S["y_psum"], 1)
                if there(i, off - 1):
                    b = number(i, off - 1)[0]
                    wait(pe, "hnt_ready", b + 1)
                    for j in range(2):
                        for c in range(DC):
                            last = pe.matmul(logit_view[:, j, :], hnt_now[:, c, P * j:P * j + P],
                                             wr[:, c, :], start=(c == 0), stop=(c == DC - 1))
                    last.then_inc(S["logits_psum"], 1)

            pipeline(pe, step)

            pe.wait_ge(S["route_dve"], MARK["earlier"])
            pe.wait_ge(S["attended"], blocks)
            for (e0, e1), bank in zip(THIRDS, (b_t, b_q, b_k)):
                at = bank[:, 0:(e1 - e0) * tiles]
                pe.matmul(at, before[:, :], chosen[:, e0:e1, 1:tiles + 1], start=True, stop=False)
                pe.matmul(at, ones[:, :], earlier[:, e0:e1, 0:tiles], start=False, stop=True)
            pe.matmul(b_v[:, 0:EXPERTS], ones[:, :], earlier[:, :, tiles], start=True, stop=True)
            pe.matmul(b_o[0:EXPERTS, 0:1], earlier[:, :, tiles], ones[:, 0:1], start=True, stop=True) \
                .then_inc(S["route_pe"], 1)
            pe.wait_ge(S["route_dve"], MARK["padded_c"])
            pe.matmul(b_y[0:EXPERTS, 0:1], upto[:, :], padded_c[:, :], start=True, stop=True) \
                .then_inc(S["route_pe"], 1)
            pe.wait_ge(S["route_dve"], MARK["past"])
            pe.matmul(b_v[0:1, 0:slot_tiles], ones[0:EXPERTS, 0:1], past[:, :], start=True, stop=True) \
                .then_inc(S["route_pe"], 1)
            pe.matmul(b_s[:, 0:slot_tiles], ones_h[:, :], zeros[:, :], start=True, stop=False)

            def place(t, u):
                wait(pe, "hot_ready", t + 1)
                for k in range(TOP):
                    last = pe.matmul(b_s[:, 0:slot_tiles], row_hot[:, u, k, :], tile_hot[:, u, k, :],
                                     start=False, stop=False)
                last.then_inc(S["hot_used"], 1)

            with pe.Fori(0, tiles // 2) as i:
                place(2 * i, 0)
                place(2 * i + 1, 1)
            pe.matmul(b_s[:, 0:slot_tiles], ones_h[:, :], zeros[:, :], start=False, stop=True) \
                .then_inc(S["route_pe"], 1)

            pe.wait_ge(S["tables_ready"], 2)
            pe.wait_ge(S["expert_w"], 16 * blocks)
            pe.wait_ge(S["down_w"], 16)

            def expert_transpose(i, u):
                pair = XG * i + u
                pe.wait_ge(gather_in[u], 32 * (i + 1))
                for s in range(2):
                    for c in range(DC):
                        at = 256 * s + P * c
                        last = pe.transpose(b_t[:, at:at + P], gathered[u][:, s, P * c:P * c + P],
                                            ident[:, :])
                last.then_inc(S["gt_psum"], 1)

            def experts_of(i):
                _, values = nc.values_load_multi_w_load_instructions(
                    tile_expert[0:1, bass.ds(2 * XG * i, 2 * XG + 2)], engines=[mybir.EngineType.PE],
                    min_val=0, max_val=EXPERTS - 1)
                return values

            def expert_up(pair, e):
                wait(pe, "gt_ready", pair + 1)
                for s in range(2):
                    for c in range(DC):
                        last = pe.matmul(gu_view[:, s, :], gt[:, s, c, :],
                                         w_gu[:, c, bass.ds(e[s], 1), :]
                                         .rearrange("p e f -> p (e f)"),
                                         start=(c == 0), stop=(c == DC - 1))
                last.then_inc(S["gu_psum"], 1)

            def expert_down(pair, e):
                wait(pe, "down_ready", pair)
                wait(pe, "act_et_ready", pair + 1)
                for s in range(2):
                    last = pe.matmul(b_k[:, 256 * s:256 * s + 256], act_et[:, s, :],
                                     w_dn[:, bass.ds(e[s], 1), :].rearrange("p e d -> p (e d)"),
                                     start=True, stop=True)
                last.then_inc(S["down_psum"], 1)

            def expert_act_transpose(pair):
                wait(pe, "act_e_ready", pair + 1)
                for s in range(2):
                    last = pe.transpose(b_v[0:F, P * s:P * s + P], act_e[:, s, :], ident[:, :])
                last.then_inc(S["act_et_psum"], 1)

            def expert_turn(i, first=False, final=False):
                e = experts_of(i)
                for u in range(XG):
                    pair = XG * i + u
                    expert_up(pair, e[2 * u + 2:2 * u + 4])
                    if not (final and u == XG - 1):
                        expert_transpose(i + (u + 1) // XG, (u + 1) % XG)
                    if not (first and u == 0):
                        expert_down(pair - 1, e[2 * u:2 * u + 2])
                    expert_act_transpose(pair)
                if final:
                    expert_down(pair, e[2 * XG:2 * XG + 2])

            expert_transpose(0, 0)
            expert_turn(0, first=True)
            with pe.Fori(1, pairs // XG - 1) as i:
                expert_turn(i)
            expert_turn(pairs // XG - 1, final=True)

            pe.wait_ge(S["shared_w"], 32)
            pe.wait_ge(S["down_ready"], pairs)

            def shared(g):
                for f in range(FB):
                    n = FB * g + f
                    wait(pe, "silu_ready", n - 1)
                    for c in range(DC):
                        last = pe.matmul((b_t, b_q)[f % 2][:, :], ws_gu[:, c, P * f:P * f + P],
                                         hnt[:, c, bass.ds(512 * g, 512)],
                                         start=(c == 0), stop=(c == DC - 1))
                    last.then_inc(S["sg_psum"], 1)
                    wait(pe, "shared_act", n - 1)
                    for c in range(DC):
                        last = pe.matmul((b_k, b_v)[f % 2][:, :], ws_gu[:, c, FS + P * f:FS + P * f + P],
                                         hnt[:, c, bass.ds(512 * g, 512)],
                                         start=(c == 0), stop=(c == DC - 1))
                    last.then_inc(S["su_psum"], 1)
                wait(pe, "shared_act", FB * g + FB)
                wait(pe, "shared_added", GT * g)
                for t in range(GT):
                    for f in range(FB):
                        last = pe.matmul((b_s, b_p)[t // 2][:, 256 * (t % 2):256 * (t % 2) + 256],
                                         act_t[:, f, P * t:P * t + P], ws_d[:, f, :],
                                         start=(f == 0), stop=(f == FB - 1))
                last.then_inc(S["shared_psum"], 1)

            shared(0)
            with pe.Fori(1, groups) as g:
                shared(g)

        @block.vector
        def _(dve):
            k = S["dve_consts"]
            dve.memset(probs.rearrange("p j s k -> p (j s k)"), 0.0).then_inc(k, 1)
            dve.memset(chosen[:, :, 0:1], 0.0).then_inc(k, 1)
            dve.memset(restart[:, :, 1:tiles + 1], 1.0).then_inc(k, 1)
            dve.memset(restart[:, :, 0:1], 0.0).then_inc(k, 1)
            dve.memset(ones_h[:, :], 1.0).then_inc(k, 1)
            dve.memset(tile_expert[:, 0:2], 0).then_inc(k, 1)
            dve.wait_ge(k, DVE_CONSTS)

            def row_stats(b, src, st, st_sem, mo, mo_sem):
                for j in range(2):
                    last = dve.bn_stats(st[:, j, :], src[:, bass.ds(2 * b + j, 1), :]
                                        .rearrange("p t d -> p (t d)"))
                last.then_inc(S[st_sem], 1)
                apart(dve, b + 1, S[st_sem])
                for j in range(2):
                    last = dve.bn_aggr(mo[:, j, :], st[:, j, :])
                last.then_inc(S[mo_sem], 1)

            def normalize(b, src, mo, rs, dst, done):
                for j in range(2):
                    last = dve.tensor_scalar(dst[:, j, :], src[:, bass.ds(2 * b + j, 1), :]
                                             .rearrange("p t d -> p (t d)"), mo[:, j, 0:1],
                                             rs[:, j:j + 1], ALU.subtract, ALU.mult)
                last.then_inc(S[done], 1)

            def step(i, off):
                if there(i, off):
                    b = number(i, off)[0]
                    wait(dve, "scores_psum", b + 1)
                    scores = b_s[:, :].rearrange("p (j s k) -> p j s k", j=2, s=2)
                    for h in range(2):
                        rows = slice(SEQ * h, SEQ * h + SEQ)
                        last = dve.tensor_reduce(negmax[rows, :], scores[rows, :, :, rows], AXIS.XY,
                                                 ALU.max, negate=True)
                    last.then_inc(S["negmax_ready"], 1)
                if there(i, off - 1):
                    b, n, u = number(i, off - 1)
                    if not isinstance(n, int) or n > 0:
                        dve.wait_ge(hn_stored[u], 16 * n)
                    wait(dve, "hnt_psum", b - 1)
                    wait(dve, "h_rstd_s", b + 1)
                    normalize(b, resid, h_moments, h_rstd, hn[u], "hn_ready")
                if there(i, off + 1):
                    b = number(i, off + 1)[0]
                    wait(dve, "q_psum", b + 1)
                    dve.tensor_scalar(qt.rearrange("p c t -> p (c t)"), b_q[:, :], SCALE, None,
                                      ALU.mult).then_inc(S["qt_ready"], 1)
                    wait(dve, "k_psum", b + 1)
                    dve.tensor_copy(kt.rearrange("p c t -> p (c t)"), b_k[:, :]) \
                        .then_inc(S["kt_ready"], 1)
                if there(i, off + 2):
                    b, n, u = number(i, off + 2)
                    apart(dve, 16 * (n + 1), x_in[u])
                    row_stats(b, resid, stats, "x_stats", moments, "x_moments")
                if there(i, off + 1):
                    b, n, u = number(i, off + 1)
                    wait(dve, "o_psum", b - 1)
                    wait(dve, "v_psum", b + 1)
                    dve.tensor_copy(v_sb[u].rearrange("p j d -> p (j d)"), b_v[:, :]) \
                        .then_inc(S["v_ready"], 1)
                if there(i, off + 2):
                    b = number(i, off + 2)[0]
                    wait(dve, "xnt_psum", b)
                    wait(dve, "x_rstd", b + 1)
                    normalize(b, resid, moments, rstd, xn, "xn_ready")
                if there(i, off):
                    b = number(i, off)[0]
                    wait(dve, "probs_ready", b + 1)
                    dve.reciprocal(rinv[:, :], rowsum[:, :]).then_inc(S["rinv_ready"], 1)
                    wait(dve, "y_psum", b + 1)
                    wait(dve, "rinv_ready", b + 1)
                    for j in range(2):
                        tile = resid[:, bass.ds(2 * b + j, 1), :].rearrange("p t d -> p (t d)")
                        last = dve.scalar_tensor_tensor(tile, b_y[:, 256 * j:256 * j + 256],
                                                        rinv[:, j:j + 1], tile, ALU.mult, ALU.add)
                    last.then_inc(S["attended"], 1)
                    apart(dve, b + 1, S["attended"])
                    row_stats(b, resid, h_stats, "h_stats_s", h_moments, "h_moments_s")
                if there(i, off - 1):
                    b = number(i, off - 1)[0]
                    wait(dve, "logits_psum", b + 1)
                    dve.tensor_copy(logits[:, :, :], logit_view).then_inc(S["logits_ready"], 1)
                    wait(dve, "logits_ready", b + 1)
                    dve.tensor_copy(gate_logit[:, bass.ds(2 * b, 2)], logits[:, :, EXPERTS])
                    for j in range(2):
                        last = dve.max(top_now[:, j, :], logits[:, j, 0:EXPERTS])
                    last.then_inc(S["top_val_ready"], 1)
                    wait(dve, "top_val_ready", b + 1)
                    dve.tensor_copy(top_val[:, bass.ds(2 * b, 2), :], top_now[:, :, :])
                    for j in range(2):
                        last = dve.max_index(top_idx[:, j, :], top_now[:, j, :],
                                             logits[:, j, 0:EXPERTS])
                    last.then_inc(S["top_idx_ready"], 1)
                    wait(dve, "top_idx_ready", b + 1)
                    hot = onehot[:, bass.ds(2 * b, 2), :, :]
                    whole = [P, 2, TOP, EXPERTS]
                    dve.tensor_tensor(hot, iota_e[:, :].unsqueeze(1).unsqueeze(1).broadcast_to(whole),
                                      top_idx[:, :, 0:TOP].unsqueeze(3).broadcast_to(whole),
                                      ALU.is_equal).then_inc(S["onehot_ready"], 1)
                    wait(dve, "onehot_ready", b + 1)
                    with nc.allow_low_precision(reason="sums of 0 and 1, exact in bfloat16"):
                        dve.tensor_reduce(
                            chosen[:, :, bass.ds(2 * b + 1, 2)].rearrange("p e t -> p t e"),
                            hot.rearrange("p t k e -> p t e k"), AXIS.X, ALU.add) \
                            .then_inc(S["chosen_ready"], 1)

            pipeline(dve, step)

            made = [0]

            def made_by(ins, mark=None):
                ins.then_inc(S["route_dve"], 1)
                made[0] += 1
                if mark is not None:
                    assert MARK[mark] == made[0], (mark, made[0])
                return made[0]

            def after(count):
                dve.wait_ge(S["route_dve"], count)

            dve.wait_ge(S["chosen_ready"], blocks)
            made_by(dve.tensor_tensor_scan(earlier[:, :, :].rearrange("p e t -> p (e t)"),
                                           restart[:, :, :].rearrange("p e t -> p (e t)"),
                                           chosen[:, :, :].rearrange("p e t -> p (e t)"),
                                           0.0, ALU.mult, ALU.add), "earlier")
            made_by(dve.tensor_tensor(top_diff[:, :, :], top_val[:, :, 0:TOP],
                                      top_val[:, :, 0:1].broadcast_to([P, tiles, TOP]), ALU.subtract),
                    "diffs")
            dve.wait_ge(S["route_pe"], 1)
            made_by(dve.tensor_scalar(count_i[:, :], b_v[:, 0:EXPERTS], float(P - 1), None, ALU.add))
            n = made_by(dve.tensor_scalar(count_ci[:, :], b_o[0:EXPERTS, 0:1], float(P - 1), None,
                                          ALU.add))
            after(n)
            made_by(dve.tensor_scalar(padded_ci[:, :], count_ci[:, :], 7, 7, ALU.logical_shift_right,
                                      ALU.logical_shift_left))
            n = made_by(dve.tensor_scalar(padded_i[:, :], count_i[:, :], 7, 7, ALU.logical_shift_right,
                                          ALU.logical_shift_left))
            after(n)
            made_by(dve.tensor_copy(padded_c[:, :], padded_ci[:, :]), "padded_c")
            n = made_by(dve.tensor_copy(padded[:, :], padded_i[:, :]))
            after(n)
            n = made_by(dve.tensor_tensor_scan(ends[:, :], ones_e[:, :], padded[:, :], 0.0, ALU.mult,
                                               ALU.add))
            after(n)
            n = made_by(dve.tensor_tensor(starts[:, :], ends[:, :], padded[:, :], ALU.subtract))
            dve.wait_ge(S["route_pe"], 2)
            n = made_by(dve.tensor_copy(ends_c[:, :], b_y[0:EXPERTS, 0:1]))
            after(n)
            made_by(dve.tensor_scalar(past[:, :], iota_start[:, :], ends_c[:, :], None, ALU.is_ge),
                    "past")
            for (e0, e1), bank in zip(THIRDS, (b_t, b_q, b_k)):
                width = e1 - e0
                n = made_by(dve.tensor_tensor(
                    posoff[:, e0:e1, :],
                    bank[:, 0:width * tiles].rearrange("p (e t) -> p e t", e=width),
                    starts[:, e0:e1].unsqueeze(2).broadcast_to([P, width, tiles]), ALU.add))
            dve.wait_ge(S["route_pe"], 3)
            made_by(dve.tensor_scalar(tile_expert[:, 2:], b_v[0:1, 0:slot_tiles],
                                      float(EXPERTS - 1), None, ALU.min))
            for t0 in range(0, tiles, TC):
                after(n)
                n = made_by(dve.tensor_tensor(
                    slot_prod, onehot[:, t0:t0 + TC, :, :],
                    posoff[:, :, t0:t0 + TC].rearrange("p e t -> p t e").unsqueeze(2)
                    .broadcast_to([P, TC, TOP, EXPERTS]), ALU.mult))
                after(n)
                n = made_by(dve.tensor_reduce(slot_f[:, t0:t0 + TC, :], slot_prod, AXIS.X, ALU.add))
            after(n)
            n = made_by(dve.tensor_copy(slot[:, :, :], slot_f[:, :, :]))
            after(n)
            made_by(dve.tensor_scalar(slot_row_i[:, :, :], slot[:, :, :], P - 1, None,
                                      ALU.bitwise_and))
            n = made_by(dve.tensor_scalar(slot_tile_i[:, :, :], slot[:, :, :], 7, None,
                                          ALU.logical_shift_right))
            after(n)
            made_by(dve.tensor_copy(slot_row[:, :, :], slot_row_i[:, :, :]))
            n = made_by(dve.tensor_copy(slot_tile[:, :, :], slot_tile_i[:, :, :]))
            after(n)

            def hot(i, u):
                t = 2 * i + u
                wait(dve, "hot_used", t - 1)
                for k in range(TOP):
                    dve.tensor_scalar(row_hot[:, u, k, :], iota_row[:, :],
                                      slot_row[:, bass.ds(t, 1), k], None, ALU.is_equal)
                    last = dve.tensor_scalar(tile_hot[:, u, k, :], iota_tile[:, :],
                                             slot_tile[:, bass.ds(t, 1), k],
                                             token_id[:, bass.ds(t, 1)], ALU.is_equal, ALU.mult)
                last.then_inc(S["hot_ready"], 1)

            hot(0, 0)
            hot(0, 1)
            with dve.Fori(1, tiles // 2) as i:
                hot(i, 0)
                hot(i, 1)

            dve.wait_ge(S["route_act"], 2)
            made_by(dve.tensor_reduce(top_sum[:, :], top_exp[:, :, :], AXIS.X, ALU.add))
            n = made_by(dve.tensor_scalar(gate_den[:, :], gate_den[:, :], 1.0, None, ALU.add))
            after(n)
            made_by(dve.reciprocal(shared_gate[:, :], gate_den[:, :]))
            n = made_by(dve.reciprocal(top_rsum[:, :], top_sum[:, :]))
            after(n)
            made_by(dve.tensor_tensor(combine[:, :, :], top_exp[:, :, :],
                                      top_rsum[:, :].unsqueeze(2).broadcast_to([P, tiles, TOP]),
                                      ALU.mult))
            dve.wait_ge(S["route_pe"], 4)
            dve.tensor_scalar(slot_token[:, :], b_s[:, 0:slot_tiles], float(tokens // 2), None,
                              ALU.add).then_inc(S["tables_ready"], 2)

            def expert_act(pair):
                wait(dve, "gate_e_ready", pair + 1)
                dve.tensor_tensor(act_e, gu_view[:, :, F:2 * F], gate_e, ALU.mult) \
                    .then_inc(S["act_e_ready"], 1)

            def expert_down_copy(pair, n, u):
                if not isinstance(n, int) or n > 0:
                    dve.wait_ge(down_stored[u], 16 * n)
                wait(dve, "down_psum", pair + 1)
                dve.tensor_copy(down_e[u].rearrange("p s d -> p (s d)"), b_k[:, :]) \
                    .then_inc(S["down_ready"], 1)

            def expert_act_copy(pair):
                wait(dve, "act_et_psum", pair + 1)
                dve.tensor_copy(act_et.rearrange("p s q -> p (s q)"), b_v[0:F, 0:2 * P]) \
                    .then_inc(S["act_et_ready"], 1)

            def expert_turn(i, first=False):
                for u in range(4):
                    pair = 4 * i + u
                    expert_act(pair)
                    if not (first and u == 0):
                        expert_down_copy(pair - 1, i + (u - 1) // 4, (u - 1) % 4)
                    expert_act_copy(pair)

            expert_turn(0, first=True)
            with dve.Fori(1, pairs // 4) as i:
                expert_turn(i)
            expert_down_copy(pairs - 1, pairs // 4 - 1, 3)

            def shared(g):
                for f in range(FB):
                    n = FB * g + f
                    wait(dve, "shared_psum", g)
                    wait(dve, "silu_ready", n + 1)
                    wait(dve, "su_psum", n + 1)
                    dve.tensor_tensor(act_t[:, f, :], (b_k, b_v)[f % 2][:, :], silu_s[f % 2],
                                      ALU.mult).then_inc(S["shared_act"], 1)
                    tile = resid[:, bass.ds(n, 1), :].rearrange("p t d -> p (t d)")
                    dve.wait_ge(pick_in[f], 64 * (g + 1))
                    for j in range(TOP):
                        wait(dve, "pick_step", TOP * n + j)
                        dve.scalar_tensor_tensor(tile, picked[f][:, j, :],
                                                 combine[:, bass.ds(n, 1), j], tile,
                                                 ALU.mult, ALU.add).then_inc(S["pick_step"], 1)
                wait(dve, "shared_psum", g + 1)
                wait(dve, "pick_step", TOP * (GT * g + GT))
                for t in range(GT):
                    tile = resid[:, bass.ds(GT * g + t, 1), :].rearrange("p t d -> p (t d)")
                    dve.scalar_tensor_tensor(
                        tile, (b_s, b_p)[t // 2][:, 256 * (t % 2):256 * (t % 2) + 256],
                        shared_gate[:, bass.ds(GT * g + t, 1)], tile, ALU.mult, ALU.add) \
                        .then_inc(S["shared_added"], 1)

            shared(0)
            with dve.Fori(1, groups) as g:
                shared(g)


_OUT = ((64, 64, 256), "float32")


def kernel(x, ctx_2048, mask_BxSx4224_bf0, L0_xattn_wq, L0_xattn_wk, L0_xattn_wv, L0_xattn_wo,
           L0_ffn_router_weight, L0_ffn_w_gate, L0_ffn_w_up, L0_ffn_w_down, L0_ffn_sw_gate,
           L0_ffn_sw_up, L0_ffn_sw_down, L0_ffn_sgate_w):
    import concourse.bacc as bacc
    from concourse.bass_utils import run_bass_kernel_spmd

    def laid(a):
        return np.ascontiguousarray(a)

    width = x.shape[-1]
    xs = np.asarray(x).reshape(-1, width)
    cs = np.asarray(ctx_2048).reshape(-1, width)
    experts, _, f = L0_ffn_w_gate.shape
    gu = np.concatenate([np.asarray(L0_ffn_w_gate), np.asarray(L0_ffn_w_up)], axis=2)
    sgu = np.concatenate([np.asarray(L0_ffn_sw_gate), np.asarray(L0_ffn_sw_up)], axis=1)
    arrays = {
        "x": laid(xs),
        "ctx": laid(cs),
        "ctx_t": laid(cs.T),
        "wq_t": laid(np.asarray(L0_xattn_wq).T),
        "wk_t": laid(np.asarray(L0_xattn_wk).T),
        "wv_t": laid(np.asarray(L0_xattn_wv).T),
        "wo_t": laid(np.asarray(L0_xattn_wo).T),
        "router_t": laid(np.concatenate([np.asarray(L0_ffn_router_weight).T,
                                         np.asarray(L0_ffn_sgate_w)], axis=1)),
        "w_gate_up": laid(gu.reshape(experts, width // 128, 128, 2 * f).transpose(2, 1, 0, 3)),
        "w_down": laid(np.asarray(L0_ffn_w_down).transpose(1, 0, 2)),
        "sw_gate_up": laid(sgu.reshape(width // 128, 128, -1).transpose(1, 0, 2)),
        "sw_down": laid(np.asarray(L0_ffn_sw_down).reshape(-1, 128, width).transpose(1, 0, 2)),
    }
    nc = bacc.Bacc("TRN2", target_bir_lowering=False, num_devices=1)
    args = {name: nc.dram_tensor(name, a.shape, mybir.dt.from_np(a.dtype), kind="ExternalInput").ap()
            for name, a in arrays.items()}
    tokens = xs.shape[0]
    slots = tokens * TOP + EXPERTS * P
    normed = nc.dram_tensor("normed", (tokens, width), F32, kind="Internal").ap()
    expert_out = nc.dram_tensor("expert_out", (slots, width), F32, kind="Internal").ap()
    out = nc.dram_tensor("out", (tokens, width), F32, kind="ExternalOutput").ap()
    build_xattn_moe(nc, **args, normed=normed, expert_out=expert_out, out=out)
    r = run_bass_kernel_spmd(nc, [arrays], core_ids=[0])
    return r.results[0]["out"].reshape(_OUT[0])
```

```python
from contextlib import ExitStack

import numpy as np

import concourse.bass as bass
from concourse import mybir

ALU = mybir.AluOpType
ACT = mybir.ActivationFunctionType
AXIS = mybir.AxisListType
F32 = mybir.dt.float32
BF16 = mybir.dt.bfloat16
F16 = mybir.dt.float16
I32 = mybir.dt.int32
U32 = mybir.dt.uint32

P = 128
D = 256
DC = D // P
SEQ = 64
EXPERTS = 32
TOP = 4
F = 96
FS = 512
EPS = 1e-5
SCALE = 1.0 / 16.0


def build_xattn_moe(nc, x, ctx, ctx_t, wq_t, wk_t, wv_t, wo_t, router_t, w_gate_up, w_down,
                    sw_gate_up, sw_down, normed, expert_out, out):
    tokens = x.shape[0]
    tiles = tokens // P
    blocks = tiles // 2
    slot_tiles = tokens * TOP // P + EXPERTS
    pairs = slot_tiles // 2
    groups = tokens // 512
    GT = 4
    FB = FS // P
    XG = 4
    ACT_HOT = 2
    HB = 4
    EARLY = 2
    TC = tiles // FB
    assert tiles == 2 * FB * HB and slot_tiles % 2 == 0 and pairs % XG == 0 and blocks % 2 == 0 and blocks >= 6

    x_v = x.rearrange("(t p) d -> p t d", p=P)
    ctx_v = ctx.rearrange("(t p) d -> p t d", p=P)
    ctx_t_v = ctx_t.rearrange("(c p) t -> p c t", p=P)
    out_v = out.rearrange("(t p) d -> p t d", p=P)
    normed_v = normed.rearrange("(t p) d -> p t d", p=P)
    expert_out_v = expert_out.rearrange("(s p) d -> p s d", p=P)

    with ExitStack() as stack:
        def sb(name, shape, dt=F32):
            return stack.enter_context(nc.sbuf_tensor(name, shape, dt))

        def sem(name):
            return stack.enter_context(nc.semaphore(name))

        resid = sb("resid", [P, tiles, D])
        hnt = sb("hnt", [P, DC, tokens])
        w_gu = sb("w_gu", [P, DC, EXPERTS, 2 * F])
        ws_gu = sb("ws_gu", [P, DC, 2 * FS])
        ws_d = sb("ws_d", [P, FB, D])
        wr = sb("wr", [P, DC, EXPERTS + 1])
        ident = sb("ident", [P, P])
        arena = sb("arena", [P, 8192])
        arena2 = sb("arena2", [P, 6144])
        taken = {"arena": 0, "arena2": 0}

        def part(which, name, words):
            at = taken[name]
            taken[name] = at + words
            assert taken[name] <= which.shape[1], name
            return which[:, at:at + words]

        xn = part(arena, "arena", 2 * D).rearrange("p (j d) -> p j d", j=2)
        xnt = part(arena, "arena", DC * 256).rearrange("p (c t) -> p c t", c=DC)
        ctx_sb = [part(arena, "arena", 2 * D).rearrange("p (j d) -> p j d", j=2) for _ in range(2)]
        ctxt_sb = [part(arena, "arena", DC * 256).rearrange("p (c t) -> p c t", c=DC) for _ in range(2)]
        qt = part(arena, "arena", DC * 256).rearrange("p (c t) -> p c t", c=DC)
        kt = part(arena, "arena", DC * 256).rearrange("p (c t) -> p c t", c=DC)
        v_sb = [part(arena, "arena", 2 * D).rearrange("p (j d) -> p j d", j=2) for _ in range(2)]
        probs = part(arena, "arena", 512).rearrange("p (j s k) -> p j s k", j=2, s=2)
        probst = part(arena, "arena", 512).rearrange("p (j s q) -> p j s q", j=2, s=2)
        ot = part(arena, "arena", DC * 256).rearrange("p (c t) -> p c t", c=DC)
        hn = [part(arena, "arena", 2 * D).rearrange("p (j d) -> p j d", j=2) for _ in range(2)]

        hnt_now = part(arena, "arena", DC * 256).rearrange("p (c t) -> p c t", c=DC)

        w_dn = arena[0:F, 0:EXPERTS * D].rearrange("f (e d) -> f e d", e=EXPERTS)

        taken["arena"] = 0
        act_late = part(arena, "arena", FB * 512).rearrange("p (f t) -> p f t", f=FB)
        picked = [part(arena, "arena", TOP * D).rearrange("p (k d) -> p k d", k=TOP) for _ in range(4)]

        w_att = [part(arena2, "arena2", DC * D).rearrange("p (c e) -> p c e", c=DC) for _ in range(4)]
        wq, wk, wv, wo = w_att
        act_early = arena2[:, 0:FB * 512].rearrange("p (f t) -> p f t", f=FB)
        onehot = part(arena2, "arena2", tiles * TOP * EXPERTS // 2).bitcast(BF16) \
            .rearrange("p (t k e) -> p t k e", t=tiles, k=TOP)
        posoff = part(arena2, "arena2", EXPERTS * tiles).rearrange("p (e t) -> p e t", e=EXPERTS)
        slot_prod = part(arena2, "arena2", TC * TOP * EXPERTS) \
            .rearrange("p (t k e) -> p t k e", t=TC, k=TOP)
        tile_hot = arena2[:, taken["arena2"] - HB * TOP * slot_tiles // 2:taken["arena2"]] \
            .bitcast(F16).rearrange("p (u k s) -> p u k s", u=HB, k=TOP)
        assert HB * TOP * slot_tiles // 2 <= (EXPERTS + TC * TOP) * tiles

        taken["arena2"] = 0
        gt = part(arena2, "arena2", 2 * DC * P).rearrange("p (s c q) -> p s c q", s=2, c=DC)
        gate_e = part(arena2, "arena2", 2 * F).rearrange("p (s f) -> p s f", s=2)
        act_e = part(arena2, "arena2", 2 * F).rearrange("p (s f) -> p s f", s=2)
        act_et = part(arena2, "arena2", 2 * P)[0:F, :].rearrange("p (s q) -> p s q", s=2)
        down_e = [part(arena2, "arena2", 2 * D).rearrange("p (s d) -> p s d", s=2) for _ in range(4)]
        assert taken["arena2"] >= FB * 512
        gathered = [part(arena2, "arena2", 2 * D).rearrange("p (s d) -> p s d", s=2) for _ in range(XG)]

        stats = sb("stats", [P, 2, 6])
        moments = sb("moments", [P, 2, 2])
        var_eps = sb("var_eps", [P, 2])
        rstd = sb("rstd", [P, 2])
        h_stats = sb("h_stats", [P, 2, 6])
        h_moments = sb("h_moments", [P, 2, 2])
        h_var_eps = sb("h_var_eps", [P, 2])
        h_rstd = sb("h_rstd", [P, 2])
        neg_half = sb("neg_half", [P, 2])
        negmax = sb("negmax", [P, 2])
        rowsum = sb("rowsum", [P, 2])
        rinv = sb("rinv", [P, 2])
        logits = sb("logits", [P, 2, EXPERTS + 1])
        gate_logit = sb("gate_logit", [P, tiles])
        gate_den = sb("gate_den", [P, tiles])
        shared_gate = sb("shared_gate", [P, tiles])
        top_val = sb("top_val", [P, tiles, 8])
        top_now = sb("top_now", [P, 2, 8])
        top_idx = sb("top_idx", [P, 2, 8], U32)
        top_diff = sb("top_diff", [P, tiles, TOP])
        top_exp = sb("top_exp", [P, tiles, TOP])
        top_sum = sb("top_sum", [P, tiles])
        top_rsum = sb("top_rsum", [P, tiles])
        combine = sb("combine", [P, tiles, TOP])
        iota_e = sb("iota_e", [P, EXPERTS])
        iota_row = sb("iota_row", [P, P], F16)
        iota_tile = sb("iota_tile", [P, slot_tiles], F16)
        iota_start = sb("iota_start", [EXPERTS, slot_tiles])
        token_id = sb("token_id", [P, tiles])
        before = sb("before", [P, P], BF16)
        ones = sb("ones", [P, P], BF16)
        ones_h = sb("ones_h", [P, P], F16)
        upto = sb("upto", [EXPERTS, EXPERTS])
        zeros = sb("zeros", [P, slot_tiles], F16)
        chosen = sb("chosen", [P, EXPERTS, tiles + 1], BF16)
        restart = sb("restart", [P, EXPERTS, tiles + 1], BF16)
        earlier = sb("earlier", [P, EXPERTS, tiles + 1], BF16)
        count_i = sb("count_i", [P, EXPERTS], I32)
        padded_i = sb("padded_i", [P, EXPERTS], I32)
        padded = sb("padded", [P, EXPERTS])
        ones_e = sb("ones_e", [P, EXPERTS])
        ends = sb("ends", [P, EXPERTS])
        starts = sb("starts", [P, EXPERTS])
        count_ci = sb("count_ci", [EXPERTS, 1], I32)
        padded_ci = sb("padded_ci", [EXPERTS, 1], I32)
        padded_c = sb("padded_c", [EXPERTS, 1])
        ends_c = sb("ends_c", [EXPERTS, 1])
        past = sb("past", [EXPERTS, slot_tiles], BF16)
        tile_expert = sb("tile_expert", [1, 2 + slot_tiles], I32)
        slot_f = sb("slot_f", [P, tiles, TOP])
        slot = sb("slot", [P, tiles, TOP], I32)
        slot_row_i = sb("slot_row_i", [P, tiles, TOP], I32)
        slot_tile_i = sb("slot_tile_i", [P, tiles, TOP], I32)
        neg_slot_row = sb("neg_slot_row", [P, tiles, TOP])
        slot_tile = sb("slot_tile", [P, tiles, TOP])
        row_dist = sb("row_dist", [P, HB, ACT_HOT, P], F16)
        row_hot = sb("row_hot", [P, HB, TOP, P], F16)
        slot_token = sb("slot_token", [P, slot_tiles], I32)
        gather_idx = sb("gather_idx", [P, XG, 2], I32)
        pick_idx = sb("pick_idx", [P, 4, TOP], I32)

        psum = [stack.enter_context(nc.psum_tensor(f"bank{i}", [P, 512], F32)) for i in range(8)]
        b_t, b_q, b_k, b_v, b_s, b_p, b_o, b_y = psum

        logit_view = b_p[:, 0:2 * (EXPERTS + 1)].rearrange("p (j e) -> p j e", j=2)
        gu_view = b_q[:, 0:4 * F].rearrange("p (s f) -> p s f", s=2)
        THIRDS = [((0, 11), b_p), ((11, 22), b_o), ((22, EXPERTS), b_s)]

        S = {n: sem(n) for n in (
            "consts", "att_w", "shared_w", "expert_w", "down_w",
            "x_stats", "x_moments", "x_var", "x_rstd", "xn_ready", "xnt_psum", "xnt_ready",
            "q_psum", "qt_ready", "k_psum", "kt_ready", "v_psum", "v_ready",
            "scores_psum", "negmax_ready", "probs_ready", "probst_psum", "probst_ready",
            "o_psum", "ot_ready", "y_psum", "rinv_ready", "attended",
            "h_stats_s", "h_moments_s", "h_var_s", "h_rstd_s", "hn_ready", "hnt_psum", "hnt_ready", "hnt_kept",
            "logits_psum", "logits_ready", "top_val_ready", "top_idx_ready", "onehot_ready",
            "chosen_ready",
            "route_dve", "route_pe", "route_act", "row_dist_ready", "row_hot_ready", "hot_ready",
            "hot_free", "tables_ready",
            "idx_copied", "gt_psum", "gt_ready", "gu_psum", "gate_e_ready", "act_e_ready",
            "act_et_psum", "act_et_ready", "down_psum", "down_ready",
            "sg_psum", "su_psum", "silu_ready", "shared_act", "shared_psum", "shared_added",
            "pick_copied", "pick_step", "out_done", "dve_consts", "passed_pool",
            "passed_dve")}
        x_in = [sem(f"x_in{u}") for u in range(2)]
        ctx_in = [sem(f"ctx_in{u}") for u in range(2)]
        ctxt_in = [sem(f"ctxt_in{u}") for u in range(2)]
        hn_stored = [sem(f"hn_stored{u}") for u in range(2)]
        gather_in = [sem(f"gather_in{u}") for u in range(XG)]
        down_stored = [sem(f"down_stored{u}") for u in range(4)]
        pick_in = [sem(f"pick_in{u}") for u in range(4)]

        DVE_CONSTS = 6
        MARK = {"earlier": 1, "diffs": 2, "padded_c": 7, "past": 20, "banks_read": 23, "rows": 33}
        CONSTS = 15

        def wait(eng, name, count):
            if isinstance(count, int) and count <= 0:
                return
            eng.wait_ge(S[name], count)

        def apart(eng, count, semaphore):
            if isinstance(count, int) and count <= 0:
                return
            eng.wait_ge(semaphore, count)
            if not isinstance(count, int):
                eng.sem_inc(S["passed_pool"] if eng is nc.gpsimd else S["passed_dve"], 1)

        def there(i, off):
            return not isinstance(i, int) or 0 <= 2 * i + off < blocks

        def number(i, off):
            return 2 * i + off, i + off // 2, off % 2

        def pipeline(eng, step, first=-2, last=None):
            last = blocks if last is None else last
            for n in range(first, 3):
                step(0, n)
            loops = (blocks - 3) // 2
            with eng.Fori(1, loops) as i:
                step(i, 1)
                step(i, 2)
            for n in range(2 * loops + 1, last + 1):
                step(0, n)

        def one_hots(eng, hots, shared_step):
            with eng.Fori(0, FB // 2) as i:
                for v in range(2):
                    for u in range(2 * HB):
                        hots(4 * HB * i + (2 * HB * v + u), u % HB)
                    shared_step(2 * i + v, v)

        block = stack.enter_context(nc.Block())

        @block.sync
        def _(sp):
            sp.dma_start(resid[:, 0:2, :], x_v[:, 0:2, :]).then_inc(x_in[0], 16)

            def load(i, off):
                if not there(i, off):
                    return
                b, n, u = number(i, off)
                if not (isinstance(b, int) and b == 0):
                    if not isinstance(n, int) or n > 0:
                        sp.wait_ge(x_in[u], 16 * n)
                    sp.dma_start(resid[:, bass.ds(2 * b, 2), :], x_v[:, bass.ds(2 * b, 2), :]) \
                        .then_inc(x_in[u], 16)
                wait(sp, "scores_psum", b - 1)
                sp.dma_start(ctxt_sb[u], ctx_t_v[:, :, bass.ds(256 * b, 256)]).then_inc(ctxt_in[u], 16)
                wait(sp, "o_psum", b - 1)
                sp.dma_start(ctx_sb[u], ctx_v[:, bass.ds(2 * b, 2), :]).then_inc(ctx_in[u], 16)

            def store_hn(i, off):
                if not there(i, off):
                    return
                b, n, u = number(i, off)
                wait(sp, "hn_ready", b + 1)
                sp.dma_start(normed_v[:, bass.ds(2 * b, 2), :], hn[u]).then_inc(hn_stored[u], 16)
                e = EXPERTS // blocks
                sp.dma_start(w_gu[:, :, bass.ds(e * b, e), :], w_gate_up[:, :, bass.ds(e * b, e), :]) \
                    .then_inc(S["expert_w"], 16)

            def step(i, off):
                load(i, off + 2)
                store_hn(i, off)
                if isinstance(i, int) and off == 2:
                    sp.dma_start(ws_gu[:, :, :], sw_gate_up).then_inc(S["shared_w"], 16)
                    sp.dma_start(ws_d[:, :, :], sw_down).then_inc(S["shared_w"], 16)

            pipeline(sp, step)
            sp.wait_ge(S["logits_ready"], blocks)
            sp.wait_ge(S["hnt_kept"], blocks)
            for u in range(2):
                sp.wait_ge(hn_stored[u], 16 * (blocks // 2))
            sp.dma_start(w_dn, w_down).then_inc(S["down_w"], 16)

            with sp.Fori(0, pairs // 4) as i:
                for u in range(4):
                    sp.wait_ge(S["down_ready"], 4 * i + (u + 1))
                    sp.dma_start(expert_out_v[:, bass.ds(8 * i + 2 * u, 2), :], down_e[u]) \
                        .then_inc(down_stored[u], 16)

            with sp.Fori(0, groups) as g:
                sp.wait_ge(S["pick_step"], TOP * GT * g + TOP * GT)
                sp.dma_start(out_v[:, bass.ds(GT * g, GT), :], resid[:, bass.ds(GT * g, GT), :]) \
                    .then_inc(S["out_done"], 16)
            sp.wait_ge(S["out_done"], 16 * groups)

        @block.gpsimd
        def _(pool):
            c = S["consts"]

            pool.memset(ident[:, :], 0.0).then_inc(c, 1)
            pool.memset(before[:, :], 1.0).then_inc(c, 1)
            pool.memset(upto[:, :], 1.0).then_inc(c, 1)
            pool.wait_ge(c, 3)
            pool.affine_select(out=ident[:, :], in_=ident[:, :], compare_op=ALU.not_equal, fill=1.0,
                               base=0, pattern=[[-1, P]], channel_multiplier=1).then_inc(c, 1)
            pool.affine_select(out=before[:, :], in_=before[:, :], compare_op=ALU.is_ge, fill=0.0,
                               base=-1, pattern=[[1, P]], channel_multiplier=-1).then_inc(c, 1)
            pool.affine_select(out=upto[:, :], in_=upto[:, :], compare_op=ALU.is_ge, fill=0.0,
                               base=0, pattern=[[1, EXPERTS]], channel_multiplier=-1).then_inc(c, 1)
            pool.memset(neg_half[:, :], -0.5).then_inc(c, 1)
            pool.iota(iota_e[:, :], [[1, EXPERTS]], base=0, channel_multiplier=0,
                      allow_small_or_imprecise_dtypes=True).then_inc(c, 1)
            pool.iota(iota_row[:, :], [[1, P]], base=0, channel_multiplier=0,
                      allow_small_or_imprecise_dtypes=True).then_inc(c, 1)
            pool.iota(iota_tile[:, :], [[1, slot_tiles]], base=0, channel_multiplier=0,
                      allow_small_or_imprecise_dtypes=True).then_inc(c, 1)
            pool.iota(iota_start[:, :], [[P, slot_tiles]], base=0, channel_multiplier=0,
                      allow_small_or_imprecise_dtypes=True).then_inc(c, 1)
            pool.iota(token_id[:, :], [[P, tiles]], base=-tokens // 2, channel_multiplier=1,
                      allow_small_or_imprecise_dtypes=True).then_inc(c, 1)
            pool.memset(zeros[:, :], 0.0).then_inc(c, 1)
            pool.memset(ones[:, :], 1.0).then_inc(c, 1)
            pool.memset(ones_e[:, :], 1.0).then_inc(c, 1)
            pool.wait_ge(c, CONSTS)

            def inverse_root(n, moments_sem, moms, veps, var_sem, out_r, rstd_sem):
                apart(pool, n + 1, S[moments_sem])
                pool.tensor_scalar(veps[:, :], moms[:, :, 1], EPS, None, ALU.add).then_inc(S[var_sem], 1)
                pool.wait_ge(S[var_sem], n + 1)
                pool.tensor_tensor(out_r[:, :], veps[:, :], neg_half[:, :], ALU.pow) \
                    .then_inc(S[rstd_sem], 1)

            def step(i, off):
                if there(i, off + 2):
                    inverse_root(number(i, off + 2)[0], "x_moments", moments, var_eps, "x_var", rstd,
                                 "x_rstd")
                if there(i, off):
                    inverse_root(number(i, off)[0], "h_moments_s", h_moments, h_var_eps, "h_var_s",
                                 h_rstd, "h_rstd_s")
                if there(i, off - 1):
                    b = number(i, off - 1)[0]
                    apart(pool, b + 1, S["hnt_ready"])
                    pool.tensor_copy(hnt[:, :, bass.ds(256 * b, 256)], hnt_now) \
                        .then_inc(S["hnt_kept"], 1)

            pipeline(pool, step)

            pool.wait_ge(S["tables_ready"], 2)
            for u in range(2):
                pool.wait_ge(hn_stored[u], 16 * (blocks // 2))

            def gather(i, u):
                pair = XG * i + u
                apart(pool, 32 * i, gather_in[u])
                pool.tensor_copy(gather_idx[:, u, :], slot_token[:, bass.ds(2 * pair, 2)]) \
                    .then_inc(S["idx_copied"], 1)
                apart(pool, pair - (XG - 1), S["gt_psum"])
                apart(pool, pair + 1, S["idx_copied"])
                for s in range(2):
                    pool.indirect_dma_start(
                        out=gathered[u][:, s, :], out_offset=None, in_=normed,
                        in_offset=bass.IndirectOffsetOnAxis(ap=gather_idx[:, u, s:s + 1], axis=0),
                    ).then_inc(gather_in[u], 16)

            for u in range(XG):
                gather(0, u)
            with pool.Fori(1, pairs // XG) as i:
                for u in range(XG):
                    gather(i, u)

            for u in range(4):
                pool.wait_ge(down_stored[u], 16 * (pairs // 4))
            pool.wait_ge(S["down_psum"], pairs)

            def pick(i, u):
                t = 4 * i + u
                apart(pool, 64 * i, pick_in[u])
                pool.tensor_copy(pick_idx[:, u, :], slot[:, bass.ds(t, 1), :]
                                 .rearrange("p t k -> p (t k)")).then_inc(S["pick_copied"], 1)
                apart(pool, TOP * (t - 3), S["pick_step"])
                apart(pool, t + 1, S["pick_copied"])
                for k in range(TOP):
                    pool.indirect_dma_start(
                        out=picked[u][:, k, :], out_offset=None, in_=expert_out,
                        in_offset=bass.IndirectOffsetOnAxis(ap=pick_idx[:, u, k:k + 1], axis=0),
                    ).then_inc(pick_in[u], 16)

            for u in range(4):
                pick(0, u)
            with pool.Fori(1, tiles // 4) as i:
                for u in range(4):
                    pick(i, u)

        @block.scalar
        def _(act):
            for w, src in zip(w_att, (wq_t, wk_t, wv_t, wo_t)):
                act.dma_start(w, src.rearrange("(c p) e -> p c e", p=P)).then_inc(S["att_w"], 16)
            act.dma_start(wr[:, :, :], router_t.rearrange("(c p) e -> p c e", p=P)) \
                .then_inc(S["att_w"], 16)
            act.wait_ge(S["dve_consts"], DVE_CONSTS)

            def step(i, off):
                if there(i, off + 1):
                    b = number(i, off + 1)[0]
                    wait(act, "v_psum", b)
                    wait(act, "xnt_psum", b + 1)
                    act.copy(xnt.rearrange("p c t -> p (c t)"), b_t[:, :]).then_inc(S["xnt_ready"], 1)
                if there(i, off):
                    b = number(i, off)[0]
                    scores = b_s[:, :].rearrange("p (j s k) -> p j s k", j=2, s=2)
                    wait(act, "negmax_ready", b + 1)
                    for h in range(2):
                        rows = slice(SEQ * h, SEQ * h + SEQ)
                        for j in range(2):
                            last = act.activation(probs[rows, j, :, rows], scores[rows, j, :, rows],
                                                  ACT.Exp, bias=negmax[rows, j:j + 1],
                                                  accum_out=rowsum[rows, j:j + 1])
                    last.then_inc(S["probs_ready"], 1)
                    wait(act, "probst_psum", b + 1)
                    act.copy(probst.rearrange("p j s q -> p (j s q)"), b_p[:, :]) \
                        .then_inc(S["probst_ready"], 1)
                    wait(act, "y_psum", b)
                    wait(act, "o_psum", b + 1)
                    act.copy(ot.rearrange("p c t -> p (c t)"), b_o[:, :]).then_inc(S["ot_ready"], 1)
                if there(i, off - 1):
                    b = number(i, off - 1)[0]
                    wait(act, "logits_psum", b)
                    wait(act, "hnt_kept", b)
                    wait(act, "hnt_psum", b + 1)
                    act.copy(hnt_now.rearrange("p c t -> p (c t)"), b_t[:, :]) \
                        .then_inc(S["hnt_ready"], 1)

            pipeline(act, step)

            def shared_silu(g, f, act_t, parity=None):
                n = FB * g + f
                wait(act, "shared_psum", g)
                wait(act, "sg_psum", n + 1)
                act.activation(act_t[:, bass.ds(f, 1), :].rearrange("p f t -> p (f t)"),
                               (b_t, b_q)[f % 2 if parity is None else parity][:, :], ACT.Silu) \
                    .then_inc(S["silu_ready"], 1)

            def row_hots(t, u):
                for k in range(ACT_HOT):
                    last = act.activation(row_dist[:, u, k, :], iota_row[:, :], ACT.Abs,
                                          bias=neg_slot_row[:, bass.ds(t, 1), k])
                last.then_inc(S["row_dist_ready"], 1)
                wait(act, "hot_free", t + 1)
                wait(act, "row_dist_ready", t + 1)
                act.activation(row_hot[:, u, 0:ACT_HOT, :].rearrange("p k q -> p (k q)"),
                               row_dist[:, u, :, :].rearrange("p k q -> p (k q)"), ACT.Relu,
                               bias=ones_e[:, 0:1], scale=-1.0).then_inc(S["row_hot_ready"], 1)

            act.wait_ge(S["route_dve"], MARK["diffs"])
            act.activation(top_exp[:, :, :], top_diff[:, :, :], ACT.Exp).then_inc(S["route_act"], 1)
            act.activation(gate_den[:, :], gate_logit[:, :], ACT.Exp, scale=-1.0) \
                .then_inc(S["route_act"], 1)
            for f in range(FB):
                shared_silu(0, f, act_early)
            act.wait_ge(S["route_dve"], MARK["rows"])
            one_hots(act, row_hots, lambda f, v: shared_silu(1, f, act_early, v))

            act.wait_ge(S["tables_ready"], 2)

            def expert_gt(pair):
                wait(act, "gu_psum", pair)
                wait(act, "gt_psum", pair + 1)
                act.copy(gt.rearrange("p s c q -> p (s c q)"), b_t[:, :]).then_inc(S["gt_ready"], 1)

            def expert_silu(pair):
                wait(act, "act_e_ready", pair)
                wait(act, "gu_psum", pair + 1)
                act.activation(gate_e, gu_view[:, :, 0:F], ACT.Silu).then_inc(S["gate_e_ready"], 1)

            expert_gt(0)
            expert_silu(0)
            with act.Fori(1, pairs) as p:
                expert_gt(p)
                expert_silu(p)

            with act.Fori(EARLY, groups) as g:
                for f in range(FB):
                    shared_silu(g, f, act_late)

        @block.tensor
        def _(pe):
            pe.wait_ge(S["consts"], CONSTS)
            pe.wait_ge(S["att_w"], 16 * 5)
            pe.wait_ge(S["dve_consts"], DVE_CONSTS)

            def step(i, off):
                if there(i, off + 1):
                    b = number(i, off + 1)[0]
                    wait(pe, "xn_ready", b + 1)
                    for c in range(DC):
                        for j in range(2):
                            last = pe.transpose(b_t[:, 256 * c + P * j:256 * c + P * j + P],
                                                xn[:, j, P * c:P * c + P], ident[:, :])
                    last.then_inc(S["xnt_psum"], 1)
                if there(i, off):
                    b, n, u = number(i, off)
                    wait(pe, "qt_ready", b + 1)
                    wait(pe, "kt_ready", b + 1)
                    pe.wait_ge(ctxt_in[u], 16 * (n + 1))
                    for j in range(2):
                        for s, keys in enumerate((ctxt_sb[u], kt)):
                            at = 256 * j + P * s
                            for c in range(DC):
                                last = pe.matmul(b_s[:, at:at + P], qt[:, c, P * j:P * j + P],
                                                 keys[:, c, P * j:P * j + P],
                                                 start=(c == 0), stop=(c == DC - 1))
                    last.then_inc(S["scores_psum"], 1)
                if there(i, off + 1):
                    b = number(i, off + 1)[0]
                    wait(pe, "xnt_ready", b + 1)
                    for w, bank, name in ((wq, b_q, "q_psum"), (wk, b_k, "k_psum")):
                        for m in range(DC):
                            for c in range(DC):
                                last = pe.matmul(bank[:, 256 * m:256 * m + 256],
                                                 w[:, c, P * m:P * m + P], xnt[:, c, :],
                                                 start=(c == 0), stop=(c == DC - 1))
                        last.then_inc(S[name], 1)
                if there(i, off):
                    b = number(i, off)[0]
                    wait(pe, "logits_ready", b - 1)
                    wait(pe, "probs_ready", b + 1)
                    for j in range(2):
                        for s in range(2):
                            at = 256 * j + P * s
                            last = pe.transpose(b_p[:, at:at + P], probs[:, j, s, :], ident[:, :])
                    last.then_inc(S["probst_psum"], 1)
                if there(i, off + 1):
                    b = number(i, off + 1)[0]
                    wait(pe, "v_ready", b)
                    for j in range(2):
                        for c in range(DC):
                            last = pe.matmul(b_v[:, 256 * j:256 * j + 256],
                                             xnt[:, c, P * j:P * j + P], wv[:, c, :],
                                             start=(c == 0), stop=(c == DC - 1))
                    last.then_inc(S["v_psum"], 1)
                if there(i, off):
                    b, n, u = number(i, off)
                    wait(pe, "probst_ready", b + 1)
                    wait(pe, "v_ready", b + 1)
                    pe.wait_ge(ctx_in[u], 16 * (n + 1))
                    for c in range(DC):
                        for j in range(2):
                            at = 256 * c + P * j
                            for s, values in enumerate((ctx_sb[u], v_sb[u])):
                                last = pe.matmul(b_o[:, at:at + P], values[:, j, P * c:P * c + P],
                                                 probst[:, j, s, :], start=(s == 0), stop=(s == 1))
                    last.then_inc(S["o_psum"], 1)
                if there(i, off - 1):
                    b = number(i, off - 1)[0]
                    wait(pe, "hn_ready", b + 1)
                    for c in range(DC):
                        for j in range(2):
                            last = pe.transpose(b_t[:, 256 * c + P * j:256 * c + P * j + P],
                                                hn[number(i, off - 1)[2]][:, j, P * c:P * c + P],
                                                ident[:, :])
                    last.then_inc(S["hnt_psum"], 1)
                if there(i, off):
                    b = number(i, off)[0]
                    wait(pe, "attended", b)
                    wait(pe, "ot_ready", b + 1)
                    for j in range(2):
                        for c in range(DC):
                            last = pe.matmul(b_y[:, 256 * j:256 * j + 256],
                                             ot[:, c, P * j:P * j + P], wo[:, c, :],
                                             start=(c == 0), stop=(c == DC - 1))
                    last.then_inc(S["y_psum"], 1)
                if there(i, off - 1):
                    b = number(i, off - 1)[0]
                    wait(pe, "hnt_ready", b + 1)
                    for j in range(2):
                        for c in range(DC):
                            last = pe.matmul(logit_view[:, j, :], hnt_now[:, c, P * j:P * j + P],
                                             wr[:, c, :], start=(c == 0), stop=(c == DC - 1))
                    last.then_inc(S["logits_psum"], 1)

            pipeline(pe, step)

            def shared_products(g, f, bank, first_column, done):
                for c in range(DC):
                    at = first_column + P * f
                    last = pe.matmul(bank[:, :], ws_gu[:, c, at:at + P],
                                     hnt[:, c, bass.ds(512 * g, 512)],
                                     start=(c == 0), stop=(c == DC - 1))
                last.then_inc(S[done], 1)

            def shared_gate_up(g, f, between=None):
                n = FB * g + f
                wait(pe, "silu_ready", n - 1)
                shared_products(g, f, (b_t, b_q)[f % 2], 0, "sg_psum")
                if between is not None:
                    between()
                wait(pe, "shared_act", n - 1)
                shared_products(g, f, (b_k, b_v)[f % 2], FS, "su_psum")

            def shared_down(g, act_t):
                wait(pe, "shared_added", GT * g)
                wait(pe, "shared_act", FB * g + FB)
                for t in range(GT):
                    for f in range(FB):
                        last = pe.matmul((b_y, b_p)[t // 2][:, 256 * (t % 2):256 * (t % 2) + 256],
                                         act_t[:, f, P * t:P * t + P], ws_d[:, f, :],
                                         start=(f == 0), stop=(f == FB - 1))
                last.then_inc(S["shared_psum"], 1)

            def place(segment):
                with pe.Fori(HB * segment, HB * segment + HB) as t:
                    u = t - HB * segment
                    wait(pe, "row_hot_ready", t + 1)
                    wait(pe, "hot_ready", t + 1)
                    for k in range(TOP):
                        last = pe.matmul(b_s[:, 0:slot_tiles],
                                         row_hot[:, bass.ds(u, 1), k, :].rearrange("p u q -> p (u q)"),
                                         tile_hot[:, bass.ds(u, 1), k, :].rearrange("p u s -> p (u s)"),
                                         start=False, stop=False)
                    last.then_inc(S["hot_free"], 1)

            pe.wait_ge(S["shared_w"], 32)
            pe.wait_ge(S["hnt_kept"], 2 * EARLY)
            pe.wait_ge(S["v_ready"], blocks)
            pe.wait_ge(S["attended"], blocks)
            shared_gate_up(0, 0)

            pe.wait_ge(S["route_dve"], MARK["earlier"])
            for (e0, e1), bank in THIRDS:
                at = bank[:, 0:(e1 - e0) * tiles]
                pe.matmul(at, before[:, :], chosen[:, e0:e1, 1:tiles + 1], start=True, stop=False)
                pe.matmul(at, ones[:, :], earlier[:, e0:e1, 0:tiles], start=False, stop=True)
            pe.matmul(b_y[:, 0:EXPERTS], ones[:, :], earlier[:, :, tiles], start=True, stop=True)
            pe.matmul(b_y[0:EXPERTS, 64:65], earlier[:, :, tiles], ones[:, 0:1], start=True, stop=True) \
                .then_inc(S["route_pe"], 1)
            shared_gate_up(0, 1)
            pe.wait_ge(S["route_dve"], MARK["padded_c"])
            pe.matmul(b_y[0:EXPERTS, 0:1], upto[:, :], padded_c[:, :], start=True, stop=True) \
                .then_inc(S["route_pe"], 1)
            shared_gate_up(0, 2)
            pe.wait_ge(S["route_dve"], MARK["past"])
            pe.matmul(b_y[0:1, 0:slot_tiles], ones[0:EXPERTS, 0:1], past[:, :], start=True, stop=True) \
                .then_inc(S["route_pe"], 1)
            shared_gate_up(0, 3)
            pe.wait_ge(S["route_dve"], MARK["banks_read"])
            pe.matmul(b_s[:, 0:slot_tiles], ones_h[:, :], zeros[:, :], start=True, stop=False) \
                .then_inc(S["hot_free"], HB)
            shared_down(0, act_early)
            for f in range(FB):
                shared_gate_up(1, f, between=lambda: place(2 * f))
                place(2 * f + 1)
            pe.matmul(b_s[:, 0:slot_tiles], ones_h[:, :], zeros[:, :], start=False, stop=True) \
                .then_inc(S["route_pe"], 1)
            shared_down(1, act_early)

            pe.wait_ge(S["tables_ready"], 2)
            pe.wait_ge(S["expert_w"], 16 * blocks)
            pe.wait_ge(S["down_w"], 16)

            def expert_transpose(i, u):
                pair = XG * i + u
                pe.wait_ge(gather_in[u], 32 * (i + 1))
                for s in range(2):
                    for c in range(DC):
                        at = 256 * s + P * c
                        last = pe.transpose(b_t[:, at:at + P], gathered[u][:, s, P * c:P * c + P],
                                            ident[:, :])
                last.then_inc(S["gt_psum"], 1)

            def experts_of(first_tile, count):
                _, values = nc.values_load_multi_w_load_instructions(
                    tile_expert[0:1, bass.ds(first_tile, count)], engines=[mybir.EngineType.PE],
                    min_val=0, max_val=EXPERTS - 1,
                    skip_runtime_bounds_check_because="the table is clamped to the last expert, and "
                                                      "counts of experts are not negative")
                return values

            def expert_up(pair, e):
                wait(pe, "gt_ready", pair + 1)
                for s in range(2):
                    for c in range(DC):
                        last = pe.matmul(gu_view[:, s, :], gt[:, s, c, :],
                                         w_gu[:, c, bass.ds(e[s], 1), :]
                                         .rearrange("p e f -> p (e f)"),
                                         start=(c == 0), stop=(c == DC - 1))
                last.then_inc(S["gu_psum"], 1)

            def expert_down(pair, e):
                wait(pe, "down_ready", pair)
                wait(pe, "act_et_ready", pair + 1)
                for s in range(2):
                    last = pe.matmul(b_k[:, 256 * s:256 * s + 256], act_et[:, s, :],
                                     w_dn[:, bass.ds(e[s], 1), :].rearrange("p e d -> p (e d)"),
                                     start=True, stop=True)
                last.then_inc(S["down_psum"], 1)

            def expert_act_transpose(pair):
                wait(pe, "act_e_ready", pair + 1)
                for s in range(2):
                    last = pe.transpose(b_v[0:F, P * s:P * s + P], act_e[:, s, :], ident[:, :])
                last.then_inc(S["act_et_psum"], 1)

            def expert_turn(i, final=False):
                e = experts_of(2 * XG * i, 6)
                for u in range(XG):
                    pair = XG * i + u
                    before_e, now_e, next_e = e[0:2], e[2:4], e[4:6]
                    if not (final and u == XG - 1):
                        expert_transpose(i + (u + 1) // XG, (u + 1) % XG)
                    if not (isinstance(i, int) and i == 0 and u == 0):
                        expert_down(pair - 1, before_e)
                    expert_act_transpose(pair)
                    if not (final and u == XG - 1):
                        expert_up(pair + 1, next_e)
                    if u < XG - 1:
                        last_pair = final and u == XG - 2
                        e = e[2:6] + (() if last_pair else experts_of(2 * (XG * i + u + 3), 2))
                if final:
                    expert_down(pair, now_e)

            expert_transpose(0, 0)
            expert_up(0, experts_of(2, 2))
            expert_turn(0)
            with pe.Fori(1, pairs // XG - 1) as i:
                expert_turn(i)
            expert_turn(pairs // XG - 1, final=True)

            pe.wait_ge(S["down_ready"], pairs)
            with pe.Fori(EARLY, groups) as g:
                for f in range(FB):
                    shared_gate_up(g, f)
                shared_down(g, act_late)

        @block.vector
        def _(dve):
            k = S["dve_consts"]
            dve.memset(probs.rearrange("p j s k -> p (j s k)"), 0.0).then_inc(k, 1)
            dve.memset(chosen[:, :, 0:1], 0.0).then_inc(k, 1)
            dve.memset(restart[:, :, 1:tiles + 1], 1.0).then_inc(k, 1)
            dve.memset(restart[:, :, 0:1], 0.0).then_inc(k, 1)
            dve.memset(ones_h[:, :], 1.0).then_inc(k, 1)
            dve.memset(tile_expert[:, 0:2], 0).then_inc(k, 1)
            dve.wait_ge(k, DVE_CONSTS)

            def row_stats(b, src, st, st_sem, mo, mo_sem):
                for j in range(2):
                    last = dve.bn_stats(st[:, j, :], src[:, bass.ds(2 * b + j, 1), :]
                                        .rearrange("p t d -> p (t d)"))
                last.then_inc(S[st_sem], 1)
                apart(dve, b + 1, S[st_sem])
                for j in range(2):
                    last = dve.bn_aggr(mo[:, j, :], st[:, j, :])
                last.then_inc(S[mo_sem], 1)

            def normalize(b, src, mo, rs, dst, done):
                for j in range(2):
                    last = dve.tensor_scalar(dst[:, j, :], src[:, bass.ds(2 * b + j, 1), :]
                                             .rearrange("p t d -> p (t d)"), mo[:, j, 0:1],
                                             rs[:, j:j + 1], ALU.subtract, ALU.mult)
                last.then_inc(S[done], 1)

            def step(i, off):
                if there(i, off):
                    b = number(i, off)[0]
                    wait(dve, "scores_psum", b + 1)
                    scores = b_s[:, :].rearrange("p (j s k) -> p j s k", j=2, s=2)
                    for h in range(2):
                        rows = slice(SEQ * h, SEQ * h + SEQ)
                        last = dve.tensor_reduce(negmax[rows, :], scores[rows, :, :, rows], AXIS.XY,
                                                 ALU.max, negate=True)
                    last.then_inc(S["negmax_ready"], 1)
                if there(i, off - 1):
                    b, n, u = number(i, off - 1)
                    if not isinstance(n, int) or n > 0:
                        dve.wait_ge(hn_stored[u], 16 * n)
                    wait(dve, "hnt_psum", b - 1)
                    wait(dve, "h_rstd_s", b + 1)
                    normalize(b, resid, h_moments, h_rstd, hn[u], "hn_ready")
                if there(i, off + 1):
                    b = number(i, off + 1)[0]
                    wait(dve, "q_psum", b + 1)
                    dve.tensor_scalar(qt.rearrange("p c t -> p (c t)"), b_q[:, :], SCALE, None,
                                      ALU.mult).then_inc(S["qt_ready"], 1)
                    wait(dve, "k_psum", b + 1)
                    dve.tensor_copy(kt.rearrange("p c t -> p (c t)"), b_k[:, :]) \
                        .then_inc(S["kt_ready"], 1)
                if there(i, off + 2):
                    b, n, u = number(i, off + 2)
                    apart(dve, 16 * (n + 1), x_in[u])
                    row_stats(b, resid, stats, "x_stats", moments, "x_moments")
                if there(i, off + 1):
                    b, n, u = number(i, off + 1)
                    wait(dve, "o_psum", b - 1)
                    wait(dve, "v_psum", b + 1)
                    dve.tensor_copy(v_sb[u].rearrange("p j d -> p (j d)"), b_v[:, :]) \
                        .then_inc(S["v_ready"], 1)
                if there(i, off + 2):
                    b = number(i, off + 2)[0]
                    wait(dve, "xnt_psum", b)
                    wait(dve, "x_rstd", b + 1)
                    normalize(b, resid, moments, rstd, xn, "xn_ready")
                if there(i, off):
                    b = number(i, off)[0]
                    wait(dve, "probs_ready", b + 1)
                    dve.reciprocal(rinv[:, :], rowsum[:, :]).then_inc(S["rinv_ready"], 1)
                    wait(dve, "y_psum", b + 1)
                    wait(dve, "rinv_ready", b + 1)
                    for j in range(2):
                        tile = resid[:, bass.ds(2 * b + j, 1), :].rearrange("p t d -> p (t d)")
                        last = dve.scalar_tensor_tensor(tile, b_y[:, 256 * j:256 * j + 256],
                                                        rinv[:, j:j + 1], tile, ALU.mult, ALU.add)
                    last.then_inc(S["attended"], 1)
                    apart(dve, b + 1, S["attended"])
                    row_stats(b, resid, h_stats, "h_stats_s", h_moments, "h_moments_s")
                if there(i, off - 1):
                    b = number(i, off - 1)[0]
                    wait(dve, "logits_psum", b + 1)
                    dve.tensor_copy(logits[:, :, :], logit_view).then_inc(S["logits_ready"], 1)
                    wait(dve, "logits_ready", b + 1)
                    dve.tensor_copy(gate_logit[:, bass.ds(2 * b, 2)], logits[:, :, EXPERTS])
                    for j in range(2):
                        last = dve.max(top_now[:, j, :], logits[:, j, 0:EXPERTS])
                    last.then_inc(S["top_val_ready"], 1)
                    wait(dve, "top_val_ready", b + 1)
                    dve.tensor_copy(top_val[:, bass.ds(2 * b, 2), :], top_now[:, :, :])
                    for j in range(2):
                        last = dve.max_index(top_idx[:, j, :], top_now[:, j, :],
                                             logits[:, j, 0:EXPERTS])
                    last.then_inc(S["top_idx_ready"], 1)
                    wait(dve, "top_idx_ready", b + 1)
                    hot = onehot[:, bass.ds(2 * b, 2), :, :]
                    whole = [P, 2, TOP, EXPERTS]
                    dve.tensor_tensor(hot, iota_e[:, :].unsqueeze(1).unsqueeze(1).broadcast_to(whole),
                                      top_idx[:, :, 0:TOP].unsqueeze(3).broadcast_to(whole),
                                      ALU.is_equal).then_inc(S["onehot_ready"], 1)
                    wait(dve, "onehot_ready", b + 1)
                    with nc.allow_low_precision(reason="sums of 0 and 1, exact in bfloat16"):
                        dve.tensor_reduce(
                            chosen[:, :, bass.ds(2 * b + 1, 2)].rearrange("p e t -> p t e"),
                            hot.rearrange("p t k e -> p t e k"), AXIS.X, ALU.add) \
                            .then_inc(S["chosen_ready"], 1)

            pipeline(dve, step)

            made = [0]

            def made_by(ins, mark=None):
                ins.then_inc(S["route_dve"], 1)
                made[0] += 1
                if mark is not None:
                    assert MARK[mark] == made[0], (mark, made[0])
                return made[0]

            def after(count):
                dve.wait_ge(S["route_dve"], count)

            def shared_mul(g, f, act_t, parity=None):
                n = FB * g + f
                wait(dve, "silu_ready", n + 1)
                wait(dve, "su_psum", n + 1)
                part_f = act_t[:, bass.ds(f, 1), :].rearrange("p f t -> p (f t)")
                bank = (b_k, b_v)[f % 2 if parity is None else parity]
                dve.tensor_tensor(part_f, bank[:, :], part_f, ALU.mult).then_inc(S["shared_act"], 1)

            def shared_add(g):
                wait(dve, "shared_psum", g + 1)
                for t in range(GT):
                    tile = resid[:, bass.ds(GT * g + t, 1), :].rearrange("p t d -> p (t d)")
                    dve.scalar_tensor_tensor(
                        tile, (b_y, b_p)[t // 2][:, 256 * (t % 2):256 * (t % 2) + 256],
                        shared_gate[:, bass.ds(GT * g + t, 1)], tile, ALU.mult, ALU.add) \
                        .then_inc(S["shared_added"], 1)

            dve.wait_ge(S["chosen_ready"], blocks)
            made_by(dve.tensor_tensor_scan(earlier[:, :, :].rearrange("p e t -> p (e t)"),
                                           restart[:, :, :].rearrange("p e t -> p (e t)"),
                                           chosen[:, :, :].rearrange("p e t -> p (e t)"),
                                           0.0, ALU.mult, ALU.add), "earlier")
            made_by(dve.tensor_tensor(top_diff[:, :, :], top_val[:, :, 0:TOP],
                                      top_val[:, :, 0:1].broadcast_to([P, tiles, TOP]), ALU.subtract),
                    "diffs")
            dve.wait_ge(S["route_pe"], 1)
            made_by(dve.tensor_scalar(count_i[:, :], b_y[:, 0:EXPERTS], float(P - 1), None, ALU.add))
            n = made_by(dve.tensor_scalar(count_ci[:, :], b_y[0:EXPERTS, 64:65], float(P - 1), None,
                                          ALU.add))
            after(n)
            made_by(dve.tensor_scalar(padded_ci[:, :], count_ci[:, :], 7, 7, ALU.logical_shift_right,
                                      ALU.logical_shift_left))
            n = made_by(dve.tensor_scalar(padded_i[:, :], count_i[:, :], 7, 7, ALU.logical_shift_right,
                                          ALU.logical_shift_left))
            after(n)
            made_by(dve.tensor_copy(padded_c[:, :], padded_ci[:, :]), "padded_c")
            n = made_by(dve.tensor_copy(padded[:, :], padded_i[:, :]))
            after(n)
            n = made_by(dve.tensor_tensor_scan(ends[:, :], ones_e[:, :], padded[:, :], 0.0, ALU.mult,
                                               ALU.add))
            after(n)
            n = made_by(dve.tensor_tensor(starts[:, :], ends[:, :], padded[:, :], ALU.subtract))
            shared_mul(0, 0, act_early)
            after(n)
            for (e0, e1), bank in THIRDS:
                width = e1 - e0
                n = made_by(dve.tensor_tensor(
                    posoff[:, e0:e1, :],
                    bank[:, 0:width * tiles].rearrange("p (e t) -> p e t", e=width),
                    starts[:, e0:e1].unsqueeze(2).broadcast_to([P, width, tiles]), ALU.add))
            dve.wait_ge(S["route_act"], 2)
            made_by(dve.tensor_reduce(top_sum[:, :], top_exp[:, :, :], AXIS.X, ALU.add))
            n = made_by(dve.tensor_scalar(gate_den[:, :], gate_den[:, :], 1.0, None, ALU.add))
            after(n)
            made_by(dve.reciprocal(shared_gate[:, :], gate_den[:, :]))
            n = made_by(dve.reciprocal(top_rsum[:, :], top_sum[:, :]))
            after(n)
            n = made_by(dve.tensor_tensor(combine[:, :, :], top_exp[:, :, :],
                                          top_rsum[:, :].unsqueeze(2).broadcast_to([P, tiles, TOP]),
                                          ALU.mult))

            dve.wait_ge(S["route_pe"], 2)
            n = made_by(dve.tensor_copy(ends_c[:, :], b_y[0:EXPERTS, 0:1]))
            after(n)
            n = made_by(dve.tensor_scalar(past[:, :], iota_start[:, :], ends_c[:, :], None, ALU.is_ge),
                    "past")
            for f in range(FB):
                t0 = TC * f
                after(n)
                n = made_by(dve.tensor_tensor(
                    slot_prod, onehot[:, t0:t0 + TC, :, :],
                    posoff[:, :, t0:t0 + TC].rearrange("p e t -> p t e").unsqueeze(2)
                    .broadcast_to([P, TC, TOP, EXPERTS]), ALU.mult))
                after(n)
                n = made_by(dve.tensor_reduce(slot_f[:, t0:t0 + TC, :], slot_prod, AXIS.X, ALU.add))
                if f == 0:
                    shared_mul(0, 1, act_early)
                    dve.wait_ge(S["route_pe"], 3)
                    n = made_by(dve.tensor_scalar(tile_expert[:, 2:], b_y[0:1, 0:slot_tiles],
                                                  float(EXPERTS - 1), None, ALU.min), "banks_read")
                elif f < FB - 1:
                    shared_mul(0, f + 1, act_early)
            after(n)
            n = made_by(dve.tensor_copy(slot[:, :, :], slot_f[:, :, :]))
            after(n)
            made_by(dve.tensor_scalar(slot_row_i[:, :, :], slot[:, :, :], P - 1, None,
                                      ALU.bitwise_and))
            n = made_by(dve.tensor_scalar(slot_tile_i[:, :, :], slot[:, :, :], 7, None,
                                          ALU.logical_shift_right))
            after(n)
            made_by(dve.tensor_scalar(neg_slot_row[:, :, :], slot_row_i[:, :, :], -1.0, None,
                                      ALU.mult), "rows")
            n = made_by(dve.tensor_copy(slot_tile[:, :, :], slot_tile_i[:, :, :]))
            after(n)

            def hots(t, u):
                wait(dve, "hot_free", t + 1)
                for k in range(ACT_HOT, TOP):
                    dve.tensor_scalar(row_hot[:, u, k, :], iota_row[:, :],
                                      neg_slot_row[:, bass.ds(t, 1), k], 0.0, ALU.add, ALU.is_equal)
                for k in range(TOP):
                    last = dve.tensor_scalar(tile_hot[:, u, k, :], iota_tile[:, :],
                                             slot_tile[:, bass.ds(t, 1), k],
                                             token_id[:, bass.ds(t, 1)], ALU.is_equal, ALU.mult)
                last.then_inc(S["hot_ready"], 1)

            one_hots(dve, hots, lambda f, v: shared_mul(1, f, act_early, v))
            dve.wait_ge(S["route_pe"], 4)
            dve.tensor_scalar(slot_token[:, :], b_s[:, 0:slot_tiles], float(tokens // 2), None,
                              ALU.add).then_inc(S["tables_ready"], 2)
            shared_add(0)
            shared_add(1)

            def expert_act(pair):
                wait(dve, "gate_e_ready", pair + 1)
                dve.tensor_tensor(act_e, gu_view[:, :, F:2 * F], gate_e, ALU.mult) \
                    .then_inc(S["act_e_ready"], 1)

            def expert_down_copy(pair, n, u):
                if not isinstance(n, int) or n > 0:
                    dve.wait_ge(down_stored[u], 16 * n)
                wait(dve, "down_psum", pair + 1)
                dve.tensor_copy(down_e[u].rearrange("p s d -> p (s d)"), b_k[:, :]) \
                    .then_inc(S["down_ready"], 1)

            def expert_act_copy(pair):
                wait(dve, "act_et_psum", pair + 1)
                dve.tensor_copy(act_et.rearrange("p s q -> p (s q)"), b_v[0:F, 0:2 * P]) \
                    .then_inc(S["act_et_ready"], 1)

            def expert_turn(i, first=False):
                for u in range(4):
                    pair = 4 * i + u
                    expert_act(pair)
                    if not (first and u == 0):
                        expert_down_copy(pair - 1, i + (u - 1) // 4, (u - 1) % 4)
                    expert_act_copy(pair)

            expert_turn(0, first=True)
            with dve.Fori(1, pairs // 4) as i:
                expert_turn(i)
            expert_down_copy(pairs - 1, pairs // 4 - 1, 3)

            def weigh_picks(q, u):
                n = GT * q + u
                tile = resid[:, bass.ds(n, 1), :].rearrange("p t d -> p (t d)")
                wait(dve, "shared_added", n + 1)
                dve.wait_ge(pick_in[u], 64 * (q + 1))
                for j in range(TOP):
                    wait(dve, "pick_step", TOP * n + j)
                    dve.scalar_tensor_tensor(tile, picked[u][:, j, :],
                                             combine[:, bass.ds(n, 1), j], tile,
                                             ALU.mult, ALU.add).then_inc(S["pick_step"], 1)

            def turn(q):
                for f in range(FB):
                    shared_mul(q + EARLY, f, act_late)
                    weigh_picks(q, f)
                shared_add(q + EARLY)

            turn(0)
            with dve.Fori(1, groups - EARLY) as q:
                turn(q)
            with dve.Fori(groups - EARLY, groups) as q:
                for u in range(GT):
                    weigh_picks(q, u)


_OUT = ((64, 64, 256), "float32")


def kernel(x, ctx_2048, mask_BxSx4224_bf0, L0_xattn_wq, L0_xattn_wk, L0_xattn_wv, L0_xattn_wo,
           L0_ffn_router_weight, L0_ffn_w_gate, L0_ffn_w_up, L0_ffn_w_down, L0_ffn_sw_gate,
           L0_ffn_sw_up, L0_ffn_sw_down, L0_ffn_sgate_w):
    import concourse.bacc as bacc
    from concourse.bass_utils import run_bass_kernel_spmd

    def laid(a):
        return np.ascontiguousarray(a)

    width = x.shape[-1]
    xs = np.asarray(x).reshape(-1, width)
    cs = np.asarray(ctx_2048).reshape(-1, width)
    experts, _, f = L0_ffn_w_gate.shape
    gu = np.concatenate([np.asarray(L0_ffn_w_gate), np.asarray(L0_ffn_w_up)], axis=2)
    sgu = np.concatenate([np.asarray(L0_ffn_sw_gate), np.asarray(L0_ffn_sw_up)], axis=1)
    arrays = {
        "x": laid(xs),
        "ctx": laid(cs),
        "ctx_t": laid(cs.T),
        "wq_t": laid(np.asarray(L0_xattn_wq).T),
        "wk_t": laid(np.asarray(L0_xattn_wk).T),
        "wv_t": laid(np.asarray(L0_xattn_wv).T),
        "wo_t": laid(np.asarray(L0_xattn_wo).T),
        "router_t": laid(np.concatenate([np.asarray(L0_ffn_router_weight).T,
                                         np.asarray(L0_ffn_sgate_w)], axis=1)),
        "w_gate_up": laid(gu.reshape(experts, width // 128, 128, 2 * f).transpose(2, 1, 0, 3)),
        "w_down": laid(np.asarray(L0_ffn_w_down).transpose(1, 0, 2)),
        "sw_gate_up": laid(sgu.reshape(width // 128, 128, -1).transpose(1, 0, 2)),
        "sw_down": laid(np.asarray(L0_ffn_sw_down).reshape(-1, 128, width).transpose(1, 0, 2)),
    }
    nc = bacc.Bacc("TRN2", target_bir_lowering=False, num_devices=1)
    args = {name: nc.dram_tensor(name, a.shape, mybir.dt.from_np(a.dtype), kind="ExternalInput").ap()
            for name, a in arrays.items()}
    tokens = xs.shape[0]
    slots = tokens * TOP + EXPERTS * P
    normed = nc.dram_tensor("normed", (tokens, width), F32, kind="Internal").ap()
    expert_out = nc.dram_tensor("expert_out", (slots, width), F32, kind="Internal").ap()
    out = nc.dram_tensor("out", (tokens, width), F32, kind="ExternalOutput").ap()
    build_xattn_moe(nc, **args, normed=normed, expert_out=expert_out, out=out)
    r = run_bass_kernel_spmd(nc, [arrays], core_ids=[0])
    return r.results[0]["out"].reshape(_OUT[0])
```

```python
from contextlib import ExitStack

import numpy as np

import concourse.bass as bass
from concourse import mybir

ALU = mybir.AluOpType
ACT = mybir.ActivationFunctionType
AXIS = mybir.AxisListType
F32 = mybir.dt.float32
F32R = mybir.dt.float32r
BF16 = mybir.dt.bfloat16
F16 = mybir.dt.float16
I32 = mybir.dt.int32
U32 = mybir.dt.uint32

P = 128
D = 256
DC = D // P
SEQ = 64
EXPERTS = 32
TOP = 4
F = 96
FS = 512
EPS = 1e-5
SCALE = 1.0 / 16.0


def build_xattn_moe(nc, x, ctx, ctx_t, wq_t, wk_t, wv_t, wo_t, router_t, w_gate_up, w_down,
                    sw_gate_up, sw_down, normed, expert_out, out):
    tokens = x.shape[0]
    tiles = tokens // P
    blocks = tiles // 2
    slot_tiles = tokens * TOP // P + EXPERTS
    pairs = slot_tiles // 2
    groups = tokens // 512
    GT = 4
    FB = FS // P
    XG = 4
    ACT_HOT = 2
    HB = 4
    LATE = 8
    PT = 5
    EARLY = 2
    TC = tiles // FB
    assert tiles // PT == groups - EARLY and tiles % (4 * HB) == 0 and slot_tiles % 2 == 0 and pairs % XG == 0 and blocks % 2 == 0 and blocks >= 6

    x_v = x.rearrange("(t p) d -> p t d", p=P)
    ctx_v = ctx.rearrange("(t p) d -> p t d", p=P)
    ctx_t_v = ctx_t.rearrange("(c p) t -> p c t", p=P)
    out_v = out.rearrange("(t p) d -> p t d", p=P)
    normed_v = normed.rearrange("(t p) d -> p t d", p=P)
    expert_out_v = expert_out.rearrange("(s p) d -> p s d", p=P)

    with ExitStack() as stack:
        def sb(name, shape, dt=F32):
            return stack.enter_context(nc.sbuf_tensor(name, shape, dt))

        def sem(name):
            return stack.enter_context(nc.semaphore(name))

        def under(*parts):
            with ExitStack() as passing:
                return [passing.enter_context(nc.sbuf_tensor(name or f"gap_{words}_{n}", [P, words],
                                                             F32R if name else F32))
                        for n, (name, words) in enumerate(parts)]

        resid = sb("resid", [P, tiles, D])
        hnt = sb("hnt", [P, DC, tokens])
        early_words = (EXPERTS - LATE) * 2 * F
        _, w_hi_012, _, w_hi_3_rests = under(("", early_words), ("w_hi_012", 3 * DC * D),
                                             ("", early_words), ("w_hi_3_rests", 3 * DC * D))
        w_gu = sb("w_gu", [P, DC, EXPERTS, 2 * F])
        ws_gu = sb("ws_gu", [P, DC, 2 * FS])
        ws_d = sb("ws_d", [P, FB, D])
        wr = sb("wr", [P, DC, EXPERTS + 1])
        ident = sb("ident", [P, P])
        _, xnt_hi, _, ot_hi = under(("", 2 * D), ("xnt_hi", DC * 256), ("", 10 * 512), ("ot_hi", DC * 256))
        arena = sb("arena", [P, 8192])
        (w_rests,) = under(("w_rests", 4 * DC * D))
        arena2 = sb("arena2", [P, 6144])
        taken = {"arena": 0, "arena2": 0}

        def part(which, name, words):
            at = taken[name]
            taken[name] = at + words
            assert taken[name] <= which.shape[1], name
            return which[:, at:at + words]

        xn = part(arena, "arena", 2 * D).rearrange("p (j d) -> p j d", j=2)
        assert taken["arena"] == 2 * D
        part(arena, "arena", DC * 256)
        ctx_sb = [part(arena, "arena", 2 * D).rearrange("p (j d) -> p j d", j=2) for _ in range(2)]
        ctxt_sb = [part(arena, "arena", DC * 256).rearrange("p (c t) -> p c t", c=DC) for _ in range(2)]
        qt = part(arena, "arena", DC * 256).rearrange("p (c t) -> p c t", c=DC)
        kt = part(arena, "arena", DC * 256).rearrange("p (c t) -> p c t", c=DC)
        v_sb = [part(arena, "arena", 2 * D).rearrange("p (j d) -> p j d", j=2) for _ in range(2)]
        probs = part(arena, "arena", 512).rearrange("p (j s k) -> p j s k", j=2, s=2)
        probst = part(arena, "arena", 512).rearrange("p (j s q) -> p j s q", j=2, s=2)
        assert taken["arena"] == 12 * 512
        part(arena, "arena", DC * 256)
        hn = [part(arena, "arena", 2 * D).rearrange("p (j d) -> p j d", j=2) for _ in range(2)]

        hnt_now = part(arena, "arena", DC * 256).rearrange("p (c t) -> p c t", c=DC)

        w_dn = arena[0:F, 0:EXPERTS * D].rearrange("f (e d) -> f e d", e=EXPERTS)

        taken["arena"] = 0
        act_late = part(arena, "arena", FB * 512).rearrange("p (f t) -> p f t", f=FB)
        picked = [part(arena, "arena", TOP * D).rearrange("p (k d) -> p k d", k=TOP) for _ in range(PT)]

        w_att = [part(arena2, "arena2", DC * D).rearrange("p (c e) -> p c e", c=DC) for _ in range(4)]
        late = EXPERTS - LATE
        assert LATE * 2 * F == 3 * DC * D

        def by_chunk(which, n):
            return which[:, n * DC * D:(n + 1) * DC * D].rearrange("p (c e) -> p c e", c=DC)

        w_hi = [by_chunk(w_hi_012, n) for n in range(3)] + [by_chunk(w_hi_3_rests, 0)]
        w_lo = [by_chunk(w_rests, n) for n in range(4)]
        xnt_lo, ot_lo = by_chunk(w_hi_3_rests, 1), by_chunk(w_hi_3_rests, 2)
        xnt_hi, ot_hi = by_chunk(xnt_hi, 0), by_chunk(ot_hi, 0)
        act_early = arena2[:, 0:FB * 512].rearrange("p (f t) -> p f t", f=FB)
        onehot = part(arena2, "arena2", tiles * TOP * EXPERTS // 2).bitcast(BF16) \
            .rearrange("p (t k e) -> p t k e", t=tiles, k=TOP)
        posoff = part(arena2, "arena2", EXPERTS * tiles).rearrange("p (e t) -> p e t", e=EXPERTS)
        slot_prod = part(arena2, "arena2", TC * TOP * EXPERTS) \
            .rearrange("p (t k e) -> p t k e", t=TC, k=TOP)
        tile_hot = arena2[:, taken["arena2"] - HB * TOP * slot_tiles // 2:taken["arena2"]] \
            .bitcast(F16).rearrange("p (u k s) -> p u k s", u=HB, k=TOP)
        assert HB * TOP * slot_tiles // 2 <= (EXPERTS + TC * TOP) * tiles

        taken["arena2"] = 0
        gt = [part(arena2, "arena2", 2 * DC * P).rearrange("p (s c q) -> p s c q", s=2, c=DC)
              for _ in range(2)]
        gate_e = part(arena2, "arena2", 2 * F).rearrange("p (s f) -> p s f", s=2)
        act_e = part(arena2, "arena2", 2 * F).rearrange("p (s f) -> p s f", s=2)
        act_et = part(arena2, "arena2", 2 * P)[0:F, :].rearrange("p (s q) -> p s q", s=2)
        down_e = [part(arena2, "arena2", 2 * D).rearrange("p (s d) -> p s d", s=2) for _ in range(4)]
        assert taken["arena2"] >= FB * 512
        gathered = [part(arena2, "arena2", 2 * D).rearrange("p (s d) -> p s d", s=2) for _ in range(XG)]

        stats = sb("stats", [P, 2, 6])
        moments = sb("moments", [P, 2, 2])
        var_eps = sb("var_eps", [P, 2])
        rstd = sb("rstd", [P, 2])
        h_stats = sb("h_stats", [P, 2, 6])
        h_moments = sb("h_moments", [P, 2, 2])
        h_var_eps = sb("h_var_eps", [P, 2])
        h_rstd = sb("h_rstd", [P, 2])
        neg_half = sb("neg_half", [P, 2])
        first_exp = sb("first_exp", [P, 1])
        negmax = sb("negmax", [P, 2])
        rowsum = sb("rowsum", [P, 2])
        rinv = sb("rinv", [P, 2])
        logits = sb("logits", [P, 2, EXPERTS + 1])
        gate_logit = sb("gate_logit", [P, tiles])
        gate_den = sb("gate_den", [P, tiles])
        shared_gate = sb("shared_gate", [P, tiles])
        top_val = sb("top_val", [P, tiles, 8])
        top_now = sb("top_now", [P, 2, 8])
        top_idx = sb("top_idx", [P, 2, 8], U32)
        top_diff = sb("top_diff", [P, tiles, TOP])
        top_exp = sb("top_exp", [P, tiles, TOP])
        top_sum = sb("top_sum", [P, tiles])
        top_rsum = sb("top_rsum", [P, tiles])
        combine = sb("combine", [P, tiles, TOP])
        iota_e = sb("iota_e", [P, EXPERTS])
        iota_row = sb("iota_row", [P, P], F16)
        iota_tile = sb("iota_tile", [P, slot_tiles], F16)
        iota_start = sb("iota_start", [EXPERTS, slot_tiles])
        token_far = sb("token_far", [P, tiles])
        neg_token_far = sb("neg_token_far", [P, tiles])
        before = sb("before", [P, P], BF16)
        ones = sb("ones", [P, P], BF16)
        ones_h = sb("ones_h", [P, P], F16)
        upto = sb("upto", [EXPERTS, EXPERTS])
        zeros = sb("zeros", [P, 2 * slot_tiles], F16)
        chosen = sb("chosen", [P, EXPERTS, tiles + 1], BF16)
        restart = sb("restart", [P, EXPERTS, tiles + 1], BF16)
        earlier = sb("earlier", [P, EXPERTS, tiles + 1], BF16)
        count_i = sb("count_i", [P, EXPERTS], I32)
        padded_i = sb("padded_i", [P, EXPERTS], I32)
        padded = sb("padded", [P, EXPERTS])
        ones_e = sb("ones_e", [P, EXPERTS])
        ends = sb("ends", [P, EXPERTS])
        starts = sb("starts", [P, EXPERTS])
        count_ci = sb("count_ci", [EXPERTS, 1], I32)
        padded_ci = sb("padded_ci", [EXPERTS, 1], I32)
        padded_c = sb("padded_c", [EXPERTS, 1])
        ends_c = sb("ends_c", [EXPERTS, 1])
        past = sb("past", [EXPERTS, slot_tiles], BF16)
        tile_expert = sb("tile_expert", [1, 2 + slot_tiles], I32)
        slot_f = sb("slot_f", [P, tiles, TOP])
        slot = sb("slot", [P, tiles + PT, TOP], I32)
        slot_row_i = sb("slot_row_i", [P, tiles, TOP], I32)
        slot_tile_i = sb("slot_tile_i", [P, tiles, TOP], I32)
        neg_slot_row = sb("neg_slot_row", [P, tiles, TOP])
        slot_row = sb("slot_row", [P, tiles, TOP])
        slot_tile = sb("slot_tile", [P, tiles, TOP])
        row_dist = sb("row_dist", [P, HB, ACT_HOT, P], F16)
        row_hot = sb("row_hot", [P, HB, TOP, P], F16)
        assert HB * TOP * P // 2 == TC * TOP * EXPERTS
        pool_prod = row_hot[:, :, :, :].rearrange("p u k q -> p (u k q)").bitcast(F32) \
            .rearrange("p (t k e) -> p t k e", t=TC, k=TOP)
        slot_near = sb("slot_near", [P, slot_tiles])
        slot_token = sb("slot_token", [P, slot_tiles], I32)
        gather_idx = sb("gather_idx", [P, XG, 2], I32)
        pick_idx = sb("pick_idx", [P, PT, TOP], I32)

        psum = [stack.enter_context(nc.psum_tensor(f"bank{i}", [P, 512], F32)) for i in range(8)]
        b_t, b_q, b_k, b_v, b_s, b_p, b_o, b_y = psum

        logit_view = b_p[:, 0:2 * (EXPERTS + 1)].rearrange("p (j e) -> p j e", j=2)
        gt_banks = (b_t, b_o)
        gu_view = b_q[:, 0:4 * F].rearrange("p (s f) -> p s f", s=2)
        gate_banks, up_banks = (b_q, b_t), (b_k, b_v)
        THIRDS = [((0, 11), b_p), ((11, 22), b_o), ((22, EXPERTS), b_s)]

        S = {n: sem(n) for n in (
            "consts", "shared_w", "expert_w", "down_w",
            "x_stats", "x_moments", "x_var", "x_rstd", "xn_ready", "xnt_psum", "xnt_ready", "xnt_lo_ready", "w_hi_ready", "w_lo_ready",
            "q_psum", "qt_ready", "k_psum", "kt_ready", "v_psum", "v_ready",
            "scores_psum", "negmax_ready", "probs_ready", "probst_psum", "probst_ready",
            "o_psum", "ot_ready", "ot_lo_ready", "y_psum", "rinv_ready", "attended",
            "h_stats_s", "h_moments_s", "h_var_s", "h_rstd_s", "hn_ready", "hnt_psum", "hnt_ready", "hnt_kept",
            "logits_psum", "logits_ready", "top_val_ready", "top_idx_ready", "onehot_ready",
            "chosen_ready",
            "route_dve", "route_pe", "route_act", "row_dist_ready", "row_hot_ready", "hot_ready",
            "hot_free", "pool_products", "tables_ready",
            "idx_copied", "gt_psum", "gt_ready", "gu_psum", "gate_e_ready", "act_e_ready",
            "act_et_psum", "act_et_ready", "down_psum", "down_ready",
            "sg_psum", "su_psum", "silu_ready", "shared_act", "shared_psum", "shared_added",
            "pick_copied", "pick_step", "out_done", "dve_consts", "passed_pool",
            "passed_dve")}
        w_in = [sem(f"{w}_in") for w in ("wq", "wk", "wv", "wo", "router")]
        x_in = [sem(f"x_in{u}") for u in range(2)]
        ctx_in = [sem(f"ctx_in{u}") for u in range(2)]
        ctxt_in = [sem(f"ctxt_in{u}") for u in range(2)]
        hn_stored = [sem(f"hn_stored{u}") for u in range(2)]
        gather_in = [sem(f"gather_in{u}") for u in range(XG)]
        down_stored = [sem(f"down_stored{u}") for u in range(4)]
        pick_in = [sem(f"pick_in{u}") for u in range(PT)]

        DVE_CONSTS = 5
        MARK = {"earlier": 1, "diffs": 2, "padded_c": 7, "past": 17, "slots_by_expert": 13, "banks_read": 20,
                "pool_summed": 21, "rows": 28}
        CONSTS = 18
        ALL_CONSTS = 21

        def wait(eng, name, count):
            if isinstance(count, int) and count <= 0:
                return
            eng.wait_ge(S[name], count)

        def apart(eng, count, semaphore):
            if isinstance(count, int) and count <= 0:
                return
            eng.wait_ge(semaphore, count)
            if not isinstance(count, int):
                eng.sem_inc(S["passed_pool"] if eng is nc.gpsimd else S["passed_dve"], 1)

        def there(i, off):
            return not isinstance(i, int) or 0 <= 2 * i + off < blocks

        def number(i, off):
            return 2 * i + off, i + off // 2, off % 2

        def pipeline(eng, step, first=-2, last=None):
            last = blocks if last is None else last
            for n in range(first, 3):
                step(0, n)
            loops = (blocks - 3) // 2
            with eng.Fori(1, loops) as i:
                step(i, 1)
                step(i, 2)
            for n in range(2 * loops + 1, last + 1):
                step(0, n)

        def slot_products(eng, f, products):
            t0 = TC * f
            return eng.tensor_tensor(
                products, onehot[:, t0:t0 + TC, :, :],
                posoff[:, :, t0:t0 + TC].rearrange("p e t -> p t e").unsqueeze(2)
                .broadcast_to([P, TC, TOP, EXPERTS]), ALU.mult)

        block = stack.enter_context(nc.Block())

        @block.sync
        def _(sp):
            sp.dma_start(resid[:, 0:2, :], x_v[:, 0:2, :]).then_inc(x_in[0], 16)

            def load_x(i, off):
                if not there(i, off):
                    return
                b, n, u = number(i, off)
                if not isinstance(n, int) or n > 0:
                    sp.wait_ge(x_in[u], 16 * n)
                sp.dma_start(resid[:, bass.ds(2 * b, 2), :], x_v[:, bass.ds(2 * b, 2), :]) \
                    .then_inc(x_in[u], 16)

            def load_ctx_t(i, off):
                if not there(i, off):
                    return
                b, n, u = number(i, off)
                wait(sp, "scores_psum", b - 1)
                sp.dma_start(ctxt_sb[u], ctx_t_v[:, :, bass.ds(256 * b, 256)]).then_inc(ctxt_in[u], 16)

            def load_ctx(i, off):
                if not there(i, off):
                    return
                b, n, u = number(i, off)
                wait(sp, "o_psum", b - 1)
                sp.dma_start(ctx_sb[u], ctx_v[:, bass.ds(2 * b, 2), :]).then_inc(ctx_in[u], 16)

            def store_hn(i, off):
                if not there(i, off):
                    return
                b, n, u = number(i, off)
                wait(sp, "hn_ready", b + 1)
                sp.dma_start(normed_v[:, bass.ds(2 * b, 2), :], hn[u]).then_inc(hn_stored[u], 16)
                if not isinstance(b, int) or 1 <= b <= blocks - 4:
                    e = late // (blocks - 4)
                    sp.dma_start(w_gu[:, :, bass.ds(e * (b - 1), e), :],
                                 w_gate_up[:, :, bass.ds(e * (b - 1), e), :]).then_inc(S["expert_w"], 16)

            def step(i, off):
                load_x(i, off + 3)
                load_ctx_t(i, off + 2)
                load_ctx(i, off + 1)
                store_hn(i, off - 2)
                if isinstance(i, int) and off in (0, 1):
                    sp.dma_start(ws_gu[:, off, :], sw_gate_up[:, off, :]).then_inc(S["shared_w"], 16)
                if isinstance(i, int) and off == 2:
                    sp.dma_start(ws_d[:, :, :], sw_down).then_inc(S["shared_w"], 16)

            pipeline(sp, step, last=blocks + 1)
            sp.wait_ge(S["y_psum"], blocks)
            sp.dma_start(w_gu[:, :, late:EXPERTS, :], w_gate_up[:, :, late:EXPERTS, :]) \
                .then_inc(S["expert_w"], 16)
            sp.wait_ge(S["logits_ready"], blocks)
            sp.wait_ge(S["hnt_kept"], blocks)
            for u in range(2):
                sp.wait_ge(hn_stored[u], 16 * (blocks // 2))
            sp.dma_start(w_dn, w_down).then_inc(S["down_w"], 16)

            with sp.Fori(0, pairs // 4) as i:
                for u in range(4):
                    sp.wait_ge(S["down_ready"], 4 * i + (u + 1))
                    sp.dma_start(expert_out_v[:, bass.ds(8 * i + 2 * u, 2), :], down_e[u]) \
                        .then_inc(down_stored[u], 16)

            with sp.Fori(0, tiles // 2) as i:
                sp.wait_ge(S["pick_step"], 2 * TOP * i + 2 * TOP)
                sp.wait_ge(S["shared_added"], 2 * i + 2)
                sp.dma_start(out_v[:, bass.ds(2 * i, 2), :], resid[:, bass.ds(2 * i, 2), :]) \
                    .then_inc(S["out_done"], 16)
            sp.wait_ge(S["out_done"], 16 * (tiles // 2))

        @block.gpsimd
        def _(pool):
            c = S["consts"]

            pool.memset(ident[:, :], 0.0).then_inc(c, 1)
            pool.memset(before[:, :], 1.0).then_inc(c, 1)
            pool.memset(upto[:, :], 1.0).then_inc(c, 1)
            pool.wait_ge(c, 3)
            pool.affine_select(out=ident[:, :], in_=ident[:, :], compare_op=ALU.not_equal, fill=1.0,
                               base=0, pattern=[[-1, P]], channel_multiplier=1).then_inc(c, 1)
            pool.affine_select(out=before[:, :], in_=before[:, :], compare_op=ALU.is_ge, fill=0.0,
                               base=-1, pattern=[[1, P]], channel_multiplier=-1).then_inc(c, 1)
            pool.affine_select(out=upto[:, :], in_=upto[:, :], compare_op=ALU.is_ge, fill=0.0,
                               base=0, pattern=[[1, EXPERTS]], channel_multiplier=-1).then_inc(c, 1)
            pool.memset(neg_half[:, :], -0.5).then_inc(c, 1)
            pool.iota(iota_e[:, :], [[1, EXPERTS]], base=0, channel_multiplier=0,
                      allow_small_or_imprecise_dtypes=True).then_inc(c, 1)
            pool.iota(iota_row[:, :], [[1, P]], base=0, channel_multiplier=0,
                      allow_small_or_imprecise_dtypes=True).then_inc(c, 1)
            pool.iota(iota_tile[:, :], [[1, slot_tiles]], base=0, channel_multiplier=0,
                      allow_small_or_imprecise_dtypes=True).then_inc(c, 1)
            pool.iota(iota_start[:, :], [[P, slot_tiles]], base=0, channel_multiplier=0,
                      allow_small_or_imprecise_dtypes=True).then_inc(c, 1)
            pool.iota(token_far[:, 0:tiles // 2], [[-P, tiles // 2]], base=tokens // 2,
                      channel_multiplier=-1, allow_small_or_imprecise_dtypes=True).then_inc(c, 1)
            pool.iota(token_far[:, tiles // 2:], [[P, tiles // 2]], base=0,
                      channel_multiplier=1, allow_small_or_imprecise_dtypes=True).then_inc(c, 1)
            pool.iota(neg_token_far[:, 0:tiles // 2], [[P, tiles // 2]], base=-tokens // 2,
                      channel_multiplier=1, allow_small_or_imprecise_dtypes=True).then_inc(c, 1)
            pool.iota(neg_token_far[:, tiles // 2:], [[-P, tiles // 2]], base=0,
                      channel_multiplier=-1, allow_small_or_imprecise_dtypes=True).then_inc(c, 1)
            pool.memset(zeros[:, :], 0.0).then_inc(c, 1)
            pool.memset(ones[:, :], 1.0).then_inc(c, 1)
            pool.memset(ones_e[:, :], 1.0).then_inc(c, 1)
            pool.wait_ge(c, CONSTS)

            def inverse_root(n, moments_sem, moms, veps, var_sem, out_r, rstd_sem):
                apart(pool, n + 1, S[moments_sem])
                pool.tensor_scalar(veps[:, :], moms[:, :, 1], EPS, None, ALU.add).then_inc(S[var_sem], 1)
                pool.wait_ge(S[var_sem], n + 1)
                pool.tensor_tensor(out_r[:, :], veps[:, :], neg_half[:, :], ALU.pow) \
                    .then_inc(S[rstd_sem], 1)

            def step(i, off):
                if isinstance(i, int) and off == 2:
                    pool.memset(restart[:, :, 1:tiles + 1], 1.0).then_inc(c, 1)
                    pool.memset(restart[:, :, 0:1], 0.0).then_inc(c, 1)
                    pool.memset(ones_h[:, :], 1.0).then_inc(c, 1)
                if there(i, off + 2):
                    inverse_root(number(i, off + 2)[0], "x_moments", moments, var_eps, "x_var", rstd,
                                 "x_rstd")
                if there(i, off - 1):
                    inverse_root(number(i, off - 1)[0], "h_moments_s", h_moments, h_var_eps, "h_var_s",
                                 h_rstd, "h_rstd_s")
                if there(i, off - 2):
                    b = number(i, off - 2)[0]
                    apart(pool, b + 1, S["hnt_ready"])
                    pool.tensor_copy(hnt[:, :, bass.ds(256 * b, 256)], hnt_now) \
                        .then_inc(S["hnt_kept"], 1)

            pipeline(pool, step, last=blocks + 1)

            for f in range(1, FB, 2):
                pool.wait_ge(S["route_dve"], MARK["slots_by_expert"] if f == 1 else MARK["pool_summed"])
                slot_products(pool, f, pool_prod).then_inc(S["pool_products"], 1)

            pool.wait_ge(S["tables_ready"], 2)
            for u in range(2):
                pool.wait_ge(hn_stored[u], 16 * (blocks // 2))

            def gather(i, u):
                pair = XG * i + u
                apart(pool, 32 * i, gather_in[u])
                pool.tensor_copy(gather_idx[:, u, :], slot_token[:, bass.ds(2 * pair, 2)]) \
                    .then_inc(S["idx_copied"], 1)
                apart(pool, pair - (XG - 1), S["gt_psum"])
                apart(pool, pair + 1, S["idx_copied"])
                for s in range(2):
                    pool.indirect_dma_start(
                        out=gathered[u][:, s, :], out_offset=None, in_=normed,
                        in_offset=bass.IndirectOffsetOnAxis(ap=gather_idx[:, u, s:s + 1], axis=0),
                    ).then_inc(gather_in[u], 16)

            for u in range(XG):
                gather(0, u)
            with pool.Fori(1, pairs // XG) as i:
                for u in range(XG):
                    gather(i, u)

            for u in range(4):
                pool.wait_ge(down_stored[u], 16 * (pairs // 4))
            pool.wait_ge(S["down_psum"], pairs)

            def pick(i, u):
                t = PT * i + u
                apart(pool, TOP * (t - (PT - 1)), S["pick_step"])
                apart(pool, t + 1, S["pick_copied"])
                for k in range(TOP):
                    pool.indirect_dma_start(
                        out=picked[u][:, k, :], out_offset=None, in_=expert_out,
                        in_offset=bass.IndirectOffsetOnAxis(ap=pick_idx[:, u, k:k + 1], axis=0),
                    ).then_inc(pick_in[u], 16)

            for u in range(PT):
                pick(0, u)
            with pool.Fori(1, tiles // PT) as i:
                for u in range(PT):
                    pick(i, u)
            for u in range(tiles % PT):
                pick(tiles // PT, u)

        @block.scalar
        def _(act):
            for w, src, there_sem in zip((*w_att, wr[:, :, :]), (wq_t, wk_t, wv_t, wo_t, router_t), w_in):
                act.dma_start(w, src.rearrange("(c p) e -> p c e", p=P)).then_inc(there_sem, 16)
            act.wait_ge(S["dve_consts"], DVE_CONSTS)
            act.activation(first_exp[:, :], first_exp[:, :], ACT.Exp)

            def weight_hi(n):
                act.wait_ge(w_in[n], 16)
                act.copy(w_hi[n], w_att[n]).then_inc(S["w_hi_ready"], 1)

            weight_hi(0)
            weight_hi(1)

            def step(i, off):
                if there(i, off + 1):
                    b = number(i, off + 1)[0]
                    wait(act, "v_psum", b)
                    wait(act, "xnt_psum", b + 1)
                    act.copy(xnt_hi.rearrange("p c t -> p (c t)"), b_t[:, :]).then_inc(S["xnt_ready"], 1)
                    if isinstance(b, int) and b == 0:
                        weight_hi(2)
                        weight_hi(3)
                if there(i, off - 1):
                    b = number(i, off - 1)[0]
                    wait(act, "probst_psum", b + 1)
                    act.copy(probst.rearrange("p j s q -> p (j s q)"), b_p[:, :]) \
                        .then_inc(S["probst_ready"], 1)
                if there(i, off):
                    b = number(i, off)[0]
                    scores = b_s[:, :].rearrange("p (j s k) -> p j s k", j=2, s=2)
                    wait(act, "rinv_ready", b)
                    wait(act, "negmax_ready", b + 1)
                    for j in range(2):
                        for h in range(2):
                            rows = slice(SEQ * h, SEQ * h + SEQ)
                            last = act.activation(probs[rows, j, :, rows], scores[rows, j, :, rows],
                                                  ACT.Exp, bias=negmax[rows, j:j + 1],
                                                  accum_out=rowsum[rows, j:j + 1])
                    last.then_inc(S["probs_ready"], 1)
                if there(i, off + 1):
                    b = number(i, off + 1)[0]
                    wait(act, "q_psum", b + 1)
                    act.activation(qt.rearrange("p c t -> p (c t)"), b_q[:, :], ACT.Copy, scale=SCALE) \
                        .then_inc(S["qt_ready"], 1)
                if there(i, off - 1):
                    b = number(i, off - 1)[0]
                    wait(act, "y_psum", b)
                    wait(act, "o_psum", b + 1)
                    act.copy(ot_hi.rearrange("p c t -> p (c t)"), b_o[:, :]).then_inc(S["ot_ready"], 1)
                if there(i, off + 1):
                    b = number(i, off + 1)[0]
                    wait(act, "k_psum", b + 1)
                    act.copy(kt.rearrange("p c t -> p (c t)"), b_k[:, :]).then_inc(S["kt_ready"], 1)
                if there(i, off - 2):
                    b = number(i, off - 2)[0]
                    wait(act, "logits_psum", b)
                    wait(act, "hnt_kept", b)
                    wait(act, "hnt_psum", b + 1)
                    act.copy(hnt_now.rearrange("p c t -> p (c t)"), b_t[:, :]) \
                        .then_inc(S["hnt_ready"], 1)

            pipeline(act, step, last=blocks + 1)

            def shared_silu(g, f, act_t, parity=None):
                n = FB * g + f
                wait(act, "shared_psum", g)
                wait(act, "sg_psum", n + 1)
                bank = gate_banks[f % 2 if parity is None else parity]
                act.activation(act_t[:, bass.ds(f, 1), :].rearrange("p f t -> p (f t)"), bank[:, :],
                               ACT.Silu) \
                    .then_inc(S["silu_ready"], 1)

            def row_distances(t, u):
                for k in range(ACT_HOT):
                    last = act.activation(row_dist[:, u, k, :], iota_row[:, :], ACT.Abs,
                                          bias=neg_slot_row[:, bass.ds(t, 1), k])
                last.then_inc(S["row_dist_ready"], 1)

            def row_hots(t, u):
                wait(act, "hot_free", t + 1)
                wait(act, "row_dist_ready", t + 1)
                act.activation(row_hot[:, u, 0:ACT_HOT, :].rearrange("p k q -> p (k q)"),
                               row_dist[:, u, :, :].rearrange("p k q -> p (k q)"), ACT.Relu,
                               bias=token_far[:, bass.ds(t, 1)], scale=neg_token_far[:, bass.ds(t, 1)]) \
                    .then_inc(S["row_hot_ready"], 1)

            act.wait_ge(S["route_dve"], MARK["diffs"])
            act.activation(top_exp[:, :, :], top_diff[:, :, :], ACT.Exp).then_inc(S["route_act"], 1)
            act.activation(gate_den[:, :], gate_logit[:, :], ACT.Exp, scale=-1.0) \
                .then_inc(S["route_act"], 1)
            for f in range(FB):
                shared_silu(0, f, act_early)
            act.wait_ge(S["route_dve"], MARK["rows"])
            with act.Fori(0, FB // 2) as i:
                for t in range(0, tiles // 2, 2):
                    for u in range(2):
                        row_distances(tiles // 2 * i + (t + u), (t + u) % HB)
                    for u in range(2):
                        row_hots(tiles // 2 * i + (t + u), (t + u) % HB)
                for v in range(2):
                    shared_silu(1, 2 * i + v, act_early, v)

            act.wait_ge(S["tables_ready"], 2)

            def expert_gt(pair, parity):
                wait(act, "gu_psum", pair - 1)
                wait(act, "gt_psum", pair + 1)
                act.copy(gt[parity].rearrange("p s c q -> p (s c q)"), gt_banks[parity][:, :]) \
                    .then_inc(S["gt_ready"], 1)

            def expert_silu(pair):
                wait(act, "act_e_ready", pair)
                wait(act, "gu_psum", pair + 1)
                act.activation(gate_e, gu_view[:, :, 0:F], ACT.Silu).then_inc(S["gate_e_ready"], 1)

            def expert_turn(i, final=False):
                for u in range(2):
                    expert_silu(2 * i + u)
                    if not final:
                        expert_gt(2 * i + (u + 2), u)

            for u in range(2):
                expert_gt(u, u)
            expert_turn(0)
            with act.Fori(1, pairs // 2 - 1) as i:
                expert_turn(i)
            expert_turn(pairs // 2 - 1, final=True)

            with act.Fori(EARLY, groups) as g:
                for f in range(FB):
                    shared_silu(g, f, act_late)

        @block.tensor
        def _(pe):
            pe.wait_ge(S["consts"], CONSTS)
            pe.wait_ge(S["dve_consts"], DVE_CONSTS)

            def three_products(out, column, stationary, moving, late_sem=None, count=0):
                terms = [(0, 0), (0, 1), (1, 0)] if column else [(0, 0), (1, 0), (0, 1)]
                for n, (s_part, m_part) in enumerate(terms):
                    if n == 2 and late_sem is not None:
                        wait(pe, late_sem, count)
                    for c in range(DC):
                        last = pe.matmul(out, stationary(s_part, c), moving(m_part, c),
                                         start=(n == 0 and c == 0), stop=(n == 2 and c == DC - 1))
                return last

            def shared_products(g, f, bank, first_column, done):
                for c in range(DC):
                    at = first_column + P * f
                    last = pe.matmul(bank[:, :], ws_gu[:, c, at:at + P],
                                     hnt[:, c, bass.ds(512 * g, 512)],
                                     start=(c == 0), stop=(c == DC - 1))
                last.then_inc(S[done], 1)

            def shared_gate(g, f):
                wait(pe, "silu_ready", FB * g + f - 1)
                shared_products(g, f, gate_banks[f % 2], 0, "sg_psum")

            def shared_up(g, f):
                wait(pe, "shared_act", FB * g + f - 1)
                shared_products(g, f, up_banks[f % 2], FS, "su_psum")

            def projection(i, off, n, bank, name):
                if not there(i, off):
                    return
                b = number(i, off)[0]
                w = (w_hi[n], w_lo[n])
                if isinstance(b, int) and b == 0:
                    pe.wait_ge(S["w_lo_ready"], n + 1)
                wait(pe, "xnt_ready", b + 1)
                for m in range(DC):
                    last = three_products(bank[:, 256 * m:256 * m + 256], False,
                                          lambda part, c: w[part][:, c, P * m:P * m + P],
                                          lambda part, c: (xnt_hi, xnt_lo)[part][:, c, :],
                                          "xnt_lo_ready", b + 1)
                last.then_inc(S[name], 1)

            def step(i, off):
                ends = number(i, off)[0] - (blocks - 1) if isinstance(i, int) else None
                if there(i, off + 1):
                    b = number(i, off + 1)[0]
                    wait(pe, "xn_ready", b + 1)
                    for c in range(DC):
                        for j in range(2):
                            last = pe.transpose(b_t[:, 256 * c + P * j:256 * c + P * j + P],
                                                xn[:, j, P * c:P * c + P], ident[:, :])
                    last.then_inc(S["xnt_psum"], 1)
                if there(i, off):
                    b, n, u = number(i, off)
                    wait(pe, "probs_ready", b)
                    wait(pe, "qt_ready", b + 1)
                    wait(pe, "kt_ready", b + 1)
                    pe.wait_ge(ctxt_in[u], 16 * (n + 1))
                    for j in range(2):
                        for s, keys in enumerate((ctxt_sb[u], kt)):
                            at = 256 * j + P * s
                            for c in range(DC):
                                last = pe.matmul(b_s[:, at:at + P], qt[:, c, P * j:P * j + P],
                                                 keys[:, c, P * j:P * j + P],
                                                 start=(c == 0), stop=(c == DC - 1))
                    last.then_inc(S["scores_psum"], 1)
                if there(i, off - 1):
                    b = number(i, off - 1)[0]
                    wait(pe, "logits_ready", b - 1)
                    wait(pe, "probs_ready", b + 1)
                    for j in range(2):
                        for s in range(2):
                            at = 256 * j + P * s
                            last = pe.transpose(b_p[:, at:at + P], probs[:, j, s, :], ident[:, :])
                    last.then_inc(S["probst_psum"], 1)
                projection(i, off + 1, 0, b_q, "q_psum")
                if ends == 0:
                    pe.wait_ge(S["shared_w"], 16 * (DC + 1))
                    pe.wait_ge(S["hnt_kept"], 2 * EARLY)
                    shared_gate(0, 0)
                if there(i, off - 1):
                    b, n, u = number(i, off - 1)
                    wait(pe, "probst_ready", b + 1)
                    wait(pe, "v_ready", b + 1)
                    pe.wait_ge(ctx_in[u], 16 * (n + 1))
                    for c in range(DC):
                        for j in range(2):
                            at = 256 * c + P * j
                            for s, values in enumerate((ctx_sb[u], v_sb[u])):
                                last = pe.matmul(b_o[:, at:at + P], values[:, j, P * c:P * c + P],
                                                 probst[:, j, s, :], start=(s == 0), stop=(s == 1))
                    last.then_inc(S["o_psum"], 1)
                projection(i, off + 1, 1, b_k, "k_psum")
                if ends == 0:
                    shared_up(0, 0)
                if ends == 2:
                    shared_up(0, 1)
                if there(i, off - 2):
                    b, n, u = number(i, off - 2)
                    wait(pe, "hn_ready", b + 1)
                    for c in range(DC):
                        for j in range(2):
                            last = pe.transpose(b_t[:, 256 * c + P * j:256 * c + P * j + P],
                                                hn[u][:, j, P * c:P * c + P], ident[:, :])
                    last.then_inc(S["hnt_psum"], 1)
                if there(i, off - 1):
                    b = number(i, off - 1)[0]
                    wait(pe, "attended", b)
                    wait(pe, "ot_ready", b + 1)
                    if isinstance(b, int) and b == 0:
                        pe.wait_ge(S["w_lo_ready"], 4)
                    for j in range(2):
                        last = three_products(
                            b_y[:, 256 * j:256 * j + 256], True,
                            lambda part, c: (ot_hi, ot_lo)[part][:, c, P * j:P * j + P],
                            lambda part, c: (w_hi[3], w_lo[3])[part][:, c, :],
                            "ot_lo_ready", b + 1)
                    last.then_inc(S["y_psum"], 1)
                if there(i, off + 1):
                    b = number(i, off + 1)[0]
                    wait(pe, "v_ready", b)
                    if isinstance(b, int) and b == 0:
                        pe.wait_ge(S["w_lo_ready"], 3)
                    for j in range(2):
                        last = three_products(
                            b_v[:, 256 * j:256 * j + 256], True,
                            lambda part, c: (xnt_hi, xnt_lo)[part][:, c, P * j:P * j + P],
                            lambda part, c: (w_hi[2], w_lo[2])[part][:, c, :])
                    last.then_inc(S["v_psum"], 1)
                if there(i, off - 2):
                    b = number(i, off - 2)[0]
                    wait(pe, "hnt_ready", b + 1)
                    if isinstance(b, int) and b == 0:
                        pe.wait_ge(w_in[4], 16)
                    for j in range(2):
                        for c in range(DC):
                            last = pe.matmul(logit_view[:, j, :], hnt_now[:, c, P * j:P * j + P],
                                             wr[:, c, :], start=(c == 0), stop=(c == DC - 1))
                    last.then_inc(S["logits_psum"], 1)

            pipeline(pe, step, last=blocks + 1)
            pe.wait_ge(S["hnt_ready"], blocks)
            shared_gate(0, 1)

            def shared_down(g, act_t, group_tiles=range(GT)):
                wait(pe, "shared_added", GT * g)
                wait(pe, "shared_act", FB * g + FB)
                for t in group_tiles:
                    for f in range(FB):
                        last = pe.matmul((b_y, b_p)[t // 2][:, 256 * (t % 2):256 * (t % 2) + 256],
                                         act_t[:, f, P * t:P * t + P], ws_d[:, f, :],
                                         start=(f == 0), stop=(f == FB - 1))
                if t == GT - 1:
                    last.then_inc(S["shared_psum"], 1)

            def place(first, end):
                side = 0 if first < tiles // 2 else slot_tiles
                with pe.Fori(first // HB, end // HB) as i:
                    for u in range(HB):
                        wait(pe, "row_hot_ready", HB * i + (u + 1))
                        wait(pe, "hot_ready", HB * i + (u + 1))
                        for k in range(TOP):
                            last = pe.matmul(b_s[:, side:side + slot_tiles], row_hot[:, u, k, :],
                                             tile_hot[:, u, k, :], start=False, stop=False)
                        last.then_inc(S["hot_free"], 1)

            pe.wait_ge(S["consts"], ALL_CONSTS)
            pe.wait_ge(S["route_dve"], MARK["earlier"])
            pe.wait_ge(S["attended"], blocks)
            for (e0, e1), bank in THIRDS:
                at = bank[:, 0:(e1 - e0) * tiles]
                pe.matmul(at, before[:, :], chosen[:, e0:e1, 1:tiles + 1], start=True, stop=False)
                pe.matmul(at, ones[:, :], earlier[:, e0:e1, 0:tiles], start=False, stop=True)
            pe.matmul(b_y[:, 0:EXPERTS], ones[:, :], earlier[:, :, tiles], start=True, stop=True)
            pe.matmul(b_y[0:EXPERTS, 64:65], earlier[:, :, tiles], ones[:, 0:1], start=True, stop=True) \
                .then_inc(S["route_pe"], 1)
            pe.wait_ge(S["route_dve"], MARK["padded_c"])
            pe.matmul(b_y[0:EXPERTS, 0:1], upto[:, :], padded_c[:, :], start=True, stop=True) \
                .then_inc(S["route_pe"], 1)
            shared_gate(0, 2)
            shared_up(0, 2)
            pe.wait_ge(S["route_dve"], MARK["past"])
            pe.matmul(b_y[0:1, 0:slot_tiles], ones[0:EXPERTS, 0:1], past[:, :], start=True, stop=True) \
                .then_inc(S["route_pe"], 1)
            shared_gate(0, 3)
            shared_up(0, 3)
            pe.wait_ge(S["route_dve"], MARK["banks_read"])
            pe.matmul(b_s[:, 0:2 * slot_tiles], ones_h[:, :], zeros[:, :], start=True, stop=False) \
                .then_inc(S["hot_free"], HB)
            for f in range(2):
                shared_gate(1, f)
                shared_up(1, f)
            for half in range(2):
                place(HB * half, HB * half + HB)
                shared_down(0, act_early, range(GT // 2 * half, GT // 2 * (half + 1)))
            place(2 * HB, tiles // 2)
            half = tiles // 2
            place(half, half + HB)
            shared_gate(1, 2)
            place(half + HB, half + 2 * HB)
            shared_up(1, 2)
            place(half + 2 * HB, half + 3 * HB)
            shared_gate(1, 3)
            shared_up(1, 3)
            place(half + 3 * HB, tiles)
            pe.matmul(b_s[:, 0:2 * slot_tiles], ones_h[:, :], zeros[:, :], start=False, stop=True) \
                .then_inc(S["route_pe"], 1)
            shared_down(1, act_early)

            pe.wait_ge(S["tables_ready"], 2)
            pe.wait_ge(S["expert_w"], 16 * (blocks - 4 + 1))
            pe.wait_ge(S["down_w"], 16)

            def expert_transpose(i, u, halves=(0, 1)):
                pe.wait_ge(gather_in[u], 32 * (i + 1))
                for s in halves:
                    for c in range(DC):
                        at = 256 * s + P * c
                        last = pe.transpose(gt_banks[u % 2][:, at:at + P],
                                            gathered[u][:, s, P * c:P * c + P], ident[:, :])
                if 1 in halves:
                    last.then_inc(S["gt_psum"], 1)

            def experts_of(first_tile, count):
                _, values = nc.values_load_multi_w_load_instructions(
                    tile_expert[0:1, bass.ds(first_tile, count)], engines=[mybir.EngineType.PE],
                    min_val=0, max_val=EXPERTS - 1,
                    skip_runtime_bounds_check_because="the table is clamped to the last expert, and "
                                                      "counts of experts are not negative")
                return values

            def expert_up(pair, parity, e):
                wait(pe, "gt_ready", pair + 1)
                for s in range(2):
                    for c in range(DC):
                        last = pe.matmul(gu_view[:, s, :], gt[parity][:, s, c, :],
                                         w_gu[:, c, bass.ds(e[s], 1), :]
                                         .rearrange("p e f -> p (e f)"),
                                         start=(c == 0), stop=(c == DC - 1))
                last.then_inc(S["gu_psum"], 1)

            def expert_down(pair, e):
                wait(pe, "down_ready", pair)
                wait(pe, "act_et_ready", pair + 1)
                for s in range(2):
                    last = pe.matmul(b_k[:, 256 * s:256 * s + 256], act_et[:, s, :],
                                     w_dn[:, bass.ds(e[s], 1), :].rearrange("p e d -> p (e d)"),
                                     start=True, stop=True)
                last.then_inc(S["down_psum"], 1)

            def expert_act_transpose(pair):
                wait(pe, "act_e_ready", pair + 1)
                for s in range(2):
                    last = pe.transpose(b_v[0:F, P * s:P * s + P], act_e[:, s, :], ident[:, :])
                last.then_inc(S["act_et_psum"], 1)

            def expert_turn(i, final=False):
                e = experts_of(2 * XG * i, 6)
                for u in range(XG):
                    pair = XG * i + u
                    before_e, now_e, next_e = e[0:2], e[2:4], e[4:6]
                    ahead = not (final and u >= XG - 2)
                    if ahead:
                        expert_transpose(i + (u + 2) // XG, (u + 2) % XG, halves=(0,))
                    if not (isinstance(i, int) and i == 0 and u == 0):
                        expert_down(pair - 1, before_e)
                    expert_act_transpose(pair)
                    if ahead:
                        expert_transpose(i + (u + 2) // XG, (u + 2) % XG, halves=(1,))
                    if not (final and u == XG - 1):
                        expert_up(pair + 1, (u + 1) % 2, next_e)
                    if u < XG - 1:
                        last_pair = final and u == XG - 2
                        e = e[2:6] + (() if last_pair else experts_of(2 * (XG * i + u + 3), 2))
                if final:
                    expert_down(pair, now_e)

            expert_transpose(0, 0)
            expert_transpose(0, 1)
            expert_up(0, 0, experts_of(2, 2))
            expert_turn(0)
            with pe.Fori(1, pairs // XG - 1) as i:
                expert_turn(i)
            expert_turn(pairs // XG - 1, final=True)

            pe.wait_ge(S["down_ready"], pairs)
            with pe.Fori(EARLY, groups) as g:
                for f in range(FB):
                    shared_gate(g, f)
                    shared_up(g, f)
                shared_down(g, act_late)

        @block.vector
        def _(dve):
            k = S["dve_consts"]
            dve.memset(first_exp[:, :], 0.0).then_inc(k, 1)
            dve.memset(probs.rearrange("p j s k -> p (j s k)"), 0.0).then_inc(k, 1)
            dve.memset(chosen[:, :, 0:1], 0.0).then_inc(k, 1)
            dve.memset(tile_expert[:, 0:2], 0).then_inc(k, 1)
            dve.memset(slot[:, tiles:, :], 0).then_inc(k, 1)
            dve.wait_ge(k, DVE_CONSTS)

            def row_stats(b, src, st, st_sem, mo, mo_sem):
                for j in range(2):
                    last = dve.bn_stats(st[:, j, :], src[:, bass.ds(2 * b + j, 1), :]
                                        .rearrange("p t d -> p (t d)"))
                last.then_inc(S[st_sem], 1)
                apart(dve, b + 1, S[st_sem])
                for j in range(2):
                    last = dve.bn_aggr(mo[:, j, :], st[:, j, :])
                last.then_inc(S[mo_sem], 1)

            def weight_lo(n):
                dve.wait_ge(S["w_hi_ready"], n + 1)
                dve.tensor_tensor(w_lo[n], w_att[n], w_hi[n].bitcast(F32), ALU.subtract) \
                    .then_inc(S["w_lo_ready"], 1)

            def normalize(b, src, mo, rs, dst, done):
                for j in range(2):
                    last = dve.tensor_scalar(dst[:, j, :], src[:, bass.ds(2 * b + j, 1), :]
                                             .rearrange("p t d -> p (t d)"), mo[:, j, 0:1],
                                             rs[:, j:j + 1], ALU.subtract, ALU.mult)
                last.then_inc(S[done], 1)

            def step(i, off):
                if there(i, off - 1):
                    b = number(i, off - 1)[0]
                    wait(dve, "attended", b)
                    wait(dve, "probs_ready", b + 1)
                    dve.reciprocal(rinv[:, :], rowsum[:, :]).then_inc(S["rinv_ready"], 1)
                if there(i, off):
                    b = number(i, off)[0]
                    wait(dve, "scores_psum", b + 1)
                    scores = b_s[:, :].rearrange("p (j s k) -> p j s k", j=2, s=2)
                    for h in range(2):
                        rows = slice(SEQ * h, SEQ * h + SEQ)
                        last = dve.tensor_reduce(negmax[rows, :], scores[rows, :, :, rows], AXIS.XY,
                                                 ALU.max, negate=True)
                    last.then_inc(S["negmax_ready"], 1)
                if there(i, off - 3):
                    b = number(i, off - 3)[0]
                    wait(dve, "top_val_ready", b + 1)
                    dve.tensor_copy(top_val[:, bass.ds(2 * b, 2), :], top_now[:, :, :])
                    for j in range(2):
                        last = dve.max_index(top_idx[:, j, :], top_now[:, j, :],
                                             logits[:, j, 0:EXPERTS])
                    last.then_inc(S["top_idx_ready"], 1)
                if there(i, off - 2):
                    b, n, u = number(i, off - 2)
                    if not isinstance(n, int) or n > 0:
                        dve.wait_ge(hn_stored[u], 16 * n)
                    wait(dve, "hnt_psum", b - 1)
                    wait(dve, "h_rstd_s", b + 1)
                    normalize(b, resid, h_moments, h_rstd, hn[u], "hn_ready")
                if there(i, off - 3):
                    b = number(i, off - 3)[0]
                    wait(dve, "top_idx_ready", b + 1)
                    hot = onehot[:, bass.ds(2 * b, 2), :, :]
                    whole = [P, 2, TOP, EXPERTS]
                    dve.tensor_tensor(hot, iota_e[:, :].unsqueeze(1).unsqueeze(1).broadcast_to(whole),
                                      top_idx[:, :, 0:TOP].unsqueeze(3).broadcast_to(whole),
                                      ALU.is_equal).then_inc(S["onehot_ready"], 1)
                if there(i, off + 2):
                    b, n, u = number(i, off + 2)
                    apart(dve, 16 * (n + 1), x_in[u])
                    row_stats(b, resid, stats, "x_stats", moments, "x_moments")
                if there(i, off - 3):
                    b = number(i, off - 3)[0]
                    wait(dve, "onehot_ready", b + 1)
                    with nc.allow_low_precision(reason="sums of 0 and 1, exact in bfloat16"):
                        dve.tensor_reduce(
                            chosen[:, :, bass.ds(2 * b + 1, 2)].rearrange("p e t -> p t e"),
                            onehot[:, bass.ds(2 * b, 2), :, :].rearrange("p t k e -> p t e k"),
                            AXIS.X, ALU.add).then_inc(S["chosen_ready"], 1)
                if there(i, off - 1):
                    b = number(i, off - 1)[0]
                    wait(dve, "ot_ready", b + 1)
                    dve.tensor_tensor(ot_lo.rearrange("p c t -> p (c t)"), b_o[:, :],
                                      ot_hi.bitcast(F32).rearrange("p c t -> p (c t)"), ALU.subtract) \
                        .then_inc(S["ot_lo_ready"], 1)
                if there(i, off + 2):
                    b = number(i, off + 2)[0]
                    wait(dve, "xnt_psum", b)
                    wait(dve, "x_rstd", b + 1)
                    normalize(b, resid, moments, rstd, xn, "xn_ready")
                if there(i, off - 1):
                    b = number(i, off - 1)[0]
                    wait(dve, "y_psum", b + 1)
                    wait(dve, "rinv_ready", b + 1)
                    for j in range(2):
                        tile = resid[:, bass.ds(2 * b + j, 1), :].rearrange("p t d -> p (t d)")
                        last = dve.scalar_tensor_tensor(tile, b_y[:, 256 * j:256 * j + 256],
                                                        rinv[:, j:j + 1], tile, ALU.mult, ALU.add)
                    last.then_inc(S["attended"], 1)
                if there(i, off + 1):
                    b, n, u = number(i, off + 1)
                    wait(dve, "o_psum", b - 1)
                    wait(dve, "v_psum", b + 1)
                    dve.tensor_copy(v_sb[u].rearrange("p j d -> p (j d)"), b_v[:, :]) \
                        .then_inc(S["v_ready"], 1)
                if there(i, off - 2):
                    b = number(i, off - 2)[0]
                    wait(dve, "logits_psum", b + 1)
                    dve.tensor_copy(logits[:, :, :], logit_view).then_inc(S["logits_ready"], 1)
                if there(i, off + 2):
                    b = number(i, off + 2)[0]
                    if isinstance(b, int) and b == 0:
                        for n in range(2):
                            weight_lo(n)
                    wait(dve, "xnt_ready", b + 1)
                    dve.tensor_tensor(xnt_lo.rearrange("p c t -> p (c t)"), b_t[:, :],
                                      xnt_hi.bitcast(F32).rearrange("p c t -> p (c t)"), ALU.subtract) \
                        .then_inc(S["xnt_lo_ready"], 1)
                    if isinstance(b, int) and b == 0:
                        for n in range(2, 4):
                            weight_lo(n)
                if there(i, off - 1):
                    b = number(i, off - 1)[0]
                    apart(dve, b + 1, S["attended"])
                    row_stats(b, resid, h_stats, "h_stats_s", h_moments, "h_moments_s")
                if there(i, off - 2):
                    b = number(i, off - 2)[0]
                    wait(dve, "logits_ready", b + 1)
                    dve.tensor_copy(gate_logit[:, bass.ds(2 * b, 2)], logits[:, :, EXPERTS])
                    for j in range(2):
                        last = dve.max(top_now[:, j, :], logits[:, j, 0:EXPERTS])
                    last.then_inc(S["top_val_ready"], 1)

            pipeline(dve, step, last=blocks + 2)

            made = [0]

            def made_by(ins, mark=None):
                ins.then_inc(S["route_dve"], 1)
                made[0] += 1
                if mark is not None:
                    assert MARK[mark] == made[0], (mark, made[0])
                return made[0]

            def after(count):
                dve.wait_ge(S["route_dve"], count)

            def shared_mul(g, f, act_t, parity=None):
                n = FB * g + f
                wait(dve, "silu_ready", n + 1)
                wait(dve, "su_psum", n + 1)
                part_f = act_t[:, bass.ds(f, 1), :].rearrange("p f t -> p (f t)")
                bank = up_banks[f % 2 if parity is None else parity]
                dve.tensor_tensor(part_f, bank[:, :], part_f, ALU.mult).then_inc(S["shared_act"], 1)

            def shared_add(g):
                wait(dve, "shared_psum", g + 1)
                for t in range(GT):
                    tile = resid[:, bass.ds(GT * g + t, 1), :].rearrange("p t d -> p (t d)")
                    dve.scalar_tensor_tensor(
                        tile, (b_y, b_p)[t // 2][:, 256 * (t % 2):256 * (t % 2) + 256],
                        shared_gate[:, bass.ds(GT * g + t, 1)], tile, ALU.mult, ALU.add) \
                        .then_inc(S["shared_added"], 1)

            dve.wait_ge(S["consts"], ALL_CONSTS)
            dve.wait_ge(S["chosen_ready"], blocks)
            made_by(dve.tensor_tensor_scan(earlier[:, :, :].rearrange("p e t -> p (e t)"),
                                           restart[:, :, :].rearrange("p e t -> p (e t)"),
                                           chosen[:, :, :].rearrange("p e t -> p (e t)"),
                                           0.0, ALU.mult, ALU.add), "earlier")
            made_by(dve.tensor_tensor(top_diff[:, :, :], top_val[:, :, 0:TOP],
                                      top_val[:, :, 0:1].broadcast_to([P, tiles, TOP]), ALU.subtract),
                    "diffs")
            dve.wait_ge(S["route_pe"], 1)
            made_by(dve.tensor_scalar(count_i[:, :], b_y[:, 0:EXPERTS], float(P - 1), None, ALU.add))
            n = made_by(dve.tensor_scalar(count_ci[:, :], b_y[0:EXPERTS, 64:65], float(P - 1), None,
                                          ALU.add))
            after(n)
            made_by(dve.tensor_scalar(padded_ci[:, :], count_ci[:, :], 7, 7, ALU.logical_shift_right,
                                      ALU.logical_shift_left))
            n = made_by(dve.tensor_scalar(padded_i[:, :], count_i[:, :], 7, 7, ALU.logical_shift_right,
                                          ALU.logical_shift_left))
            after(n)
            made_by(dve.tensor_copy(padded_c[:, :], padded_ci[:, :]), "padded_c")
            n = made_by(dve.tensor_copy(padded[:, :], padded_i[:, :]))
            after(n)
            n = made_by(dve.tensor_tensor_scan(ends[:, :], ones_e[:, :], padded[:, :], 0.0, ALU.mult,
                                               ALU.add))
            after(n)
            n = made_by(dve.tensor_tensor(starts[:, :], ends[:, :], padded[:, :], ALU.subtract))
            shared_mul(0, 0, act_early)
            after(n)
            for (e0, e1), bank in THIRDS:
                width = e1 - e0
                n = made_by(dve.tensor_tensor(
                    posoff[:, e0:e1, :],
                    bank[:, 0:width * tiles].rearrange("p (e t) -> p e t", e=width),
                    starts[:, e0:e1].unsqueeze(2).broadcast_to([P, width, tiles]), ALU.add))
            dve.wait_ge(S["route_act"], 2)
            n = made_by(dve.tensor_scalar(gate_den[:, :], gate_den[:, :], 1.0, None, ALU.add))
            after(n)
            made_by(dve.reciprocal(shared_gate[:, :], gate_den[:, :]))
            dve.wait_ge(S["route_pe"], 2)
            n = made_by(dve.tensor_copy(ends_c[:, :], b_y[0:EXPERTS, 0:1]))
            after(n)
            n = made_by(dve.tensor_scalar(past[:, :], iota_start[:, :], ends_c[:, :], None, ALU.is_ge),
                    "past")
            def slot_sums(f, products):
                return made_by(dve.tensor_reduce(slot_f[:, TC * f:TC * (f + 1), :], products, AXIS.X,
                                                 ALU.add))

            for f in range(0, FB, 2):
                after(n)
                n = made_by(slot_products(dve, f, slot_prod))
                after(n)
                n = slot_sums(f, slot_prod)
                if f == 0:
                    shared_mul(0, 1, act_early)
                    dve.wait_ge(S["route_pe"], 3)
                    made_by(dve.tensor_scalar(tile_expert[:, 2:], b_y[0:1, 0:slot_tiles],
                                              float(EXPERTS - 1), None, ALU.min), "banks_read")
                dve.wait_ge(S["pool_products"], f // 2 + 1)
                n = slot_sums(f + 1, pool_prod)
                if f == 0:
                    assert n == MARK["pool_summed"]
                    shared_mul(0, 2, act_early)
            shared_mul(0, 3, act_early)
            after(n)
            n = made_by(dve.tensor_copy(slot[:, 0:tiles, :], slot_f[:, :, :]))
            after(n)
            made_by(dve.tensor_scalar(slot_row_i[:, :, :], slot[:, 0:tiles, :], P - 1, None,
                                      ALU.bitwise_and))
            n = made_by(dve.tensor_scalar(slot_tile_i[:, :, :], slot[:, 0:tiles, :], 7, None,
                                          ALU.logical_shift_right))
            after(n)
            made_by(dve.tensor_scalar(neg_slot_row[:, :, :], slot_row_i[:, :, :], -1.0, None,
                                      ALU.mult), "rows")
            made_by(dve.tensor_copy(slot_row[:, :, :], slot_row_i[:, :, :]))
            n = made_by(dve.tensor_copy(slot_tile[:, :, :], slot_tile_i[:, :, :]))
            after(n)

            def copy_numbers(t, u):
                dve.tensor_copy(pick_idx[:, u, :], slot[:, bass.ds(t, 1), :]
                                .rearrange("p t k -> p (t k)")).then_inc(S["pick_copied"], 1)

            for u in range(PT):
                copy_numbers(u, u)

            def hots(t, u):
                wait(dve, "hot_free", t + 1)
                for k in range(ACT_HOT, TOP):
                    dve.tensor_scalar(row_hot[:, u, k, :], iota_row[:, :],
                                      slot_row[:, bass.ds(t, 1), k], token_far[:, bass.ds(t, 1)],
                                      ALU.is_equal, ALU.mult)
                for k in range(TOP):
                    last = dve.tensor_scalar(tile_hot[:, u, k, :], iota_tile[:, :],
                                             slot_tile[:, bass.ds(t, 1), k], None, ALU.is_equal)
                last.then_inc(S["hot_ready"], 1)

            with dve.Fori(0, FB // 2) as i:
                for t in range(tiles // 2):
                    hots(tiles // 2 * i + t, t % HB)
                for v in range(2):
                    shared_mul(1, 2 * i + v, act_early, v)
            dve.wait_ge(S["route_pe"], 4)
            n = made_by(dve.tensor_scalar(slot_near[:, :], b_s[:, 0:slot_tiles], -1.0,
                                          float(tokens // 2), ALU.mult, ALU.add))
            after(n)
            dve.tensor_tensor(slot_token[:, :], slot_near[:, :], b_s[:, slot_tiles:2 * slot_tiles],
                              ALU.add).then_inc(S["tables_ready"], 2)
            shared_add(0)

            def expert_act(pair):
                wait(dve, "gate_e_ready", pair + 1)
                dve.tensor_tensor(act_e, gu_view[:, :, F:2 * F], gate_e, ALU.mult) \
                    .then_inc(S["act_e_ready"], 1)

            def expert_down_copy(pair, n, u):
                if not isinstance(n, int) or n > 0:
                    dve.wait_ge(down_stored[u], 16 * n)
                wait(dve, "down_psum", pair + 1)
                dve.tensor_copy(down_e[u].rearrange("p s d -> p (s d)"), b_k[:, :]) \
                    .then_inc(S["down_ready"], 1)

            def expert_act_copy(pair):
                wait(dve, "act_et_psum", pair + 1)
                dve.tensor_copy(act_et.rearrange("p s q -> p (s q)"), b_v[0:F, 0:2 * P]) \
                    .then_inc(S["act_et_ready"], 1)

            def expert_turn(i, first=False):
                for u in range(4):
                    pair = 4 * i + u
                    expert_act(pair)
                    if not (first and u == 0):
                        expert_down_copy(pair - 1, i + (u - 1) // 4, (u - 1) % 4)
                    expert_act_copy(pair)

            expert_turn(0, first=True)
            with dve.Fori(1, pairs // 4) as i:
                expert_turn(i)
            expert_down_copy(pairs - 1, pairs // 4 - 1, 3)

            def weigh_picks(q, u, added, final=False):
                n = PT * q + u
                tile = resid[:, bass.ds(n, 1), :].rearrange("p t d -> p (t d)")
                wait(dve, "shared_added", added)
                dve.wait_ge(pick_in[u], 64 * (q + 1))
                if not final:
                    copy_numbers(n + PT, u)
                for j in range(TOP):
                    wait(dve, "pick_step", TOP * n + j)
                    dve.scalar_tensor_tensor(tile, picked[u][:, j, :],
                                             combine[:, bass.ds(n, 1), j], tile,
                                             ALU.mult, ALU.add).then_inc(S["pick_step"], 1)

            def turn(q):
                u = 0
                for f in range(FB):
                    shared_mul(q + EARLY, f, act_late)
                    while u * FB < (f + 1) * PT - FB + 1 or (f == FB - 1 and u < PT):
                        weigh_picks(q, u, GT * (q + EARLY))
                        u += 1
                wait(dve, "pick_step", TOP * PT * (q + 1))
                shared_add(q + EARLY)

            n = made_by(dve.tensor_reduce(top_sum[:, :], top_exp[:, :, :], AXIS.X, ALU.add))
            after(n)
            n = made_by(dve.reciprocal(top_rsum[:, :], top_sum[:, :]))
            after(n)
            n = made_by(dve.tensor_tensor(combine[:, :, :], top_exp[:, :, :],
                                          top_rsum[:, :].unsqueeze(2).broadcast_to([P, tiles, TOP]),
                                          ALU.mult))
            shared_add(EARLY - 1)
            after(n)
            turn(0)
            with dve.Fori(1, groups - EARLY) as q:
                turn(q)
            for u in range(tiles % PT):
                weigh_picks(tiles // PT, u, tiles, final=True)


_OUT = ((64, 64, 256), "float32")


def kernel(x, ctx_2048, mask_BxSx4224_bf0, L0_xattn_wq, L0_xattn_wk, L0_xattn_wv, L0_xattn_wo,
           L0_ffn_router_weight, L0_ffn_w_gate, L0_ffn_w_up, L0_ffn_w_down, L0_ffn_sw_gate,
           L0_ffn_sw_up, L0_ffn_sw_down, L0_ffn_sgate_w):
    import concourse.bacc as bacc
    from concourse.bass_utils import run_bass_kernel_spmd

    def laid(a):
        return np.ascontiguousarray(a)

    width = x.shape[-1]
    xs = np.asarray(x).reshape(-1, width)
    cs = np.asarray(ctx_2048).reshape(-1, width)
    experts, _, f = L0_ffn_w_gate.shape
    gu = np.concatenate([np.asarray(L0_ffn_w_gate), np.asarray(L0_ffn_w_up)], axis=2)
    sgu = np.concatenate([np.asarray(L0_ffn_sw_gate), np.asarray(L0_ffn_sw_up)], axis=1)
    arrays = {
        "x": laid(xs),
        "ctx": laid(cs),
        "ctx_t": laid(cs.T),
        "wq_t": laid(np.asarray(L0_xattn_wq).T),
        "wk_t": laid(np.asarray(L0_xattn_wk).T),
        "wv_t": laid(np.asarray(L0_xattn_wv).T),
        "wo_t": laid(np.asarray(L0_xattn_wo).T),
        "router_t": laid(np.concatenate([np.asarray(L0_ffn_router_weight).T,
                                         np.asarray(L0_ffn_sgate_w)], axis=1)),
        "w_gate_up": laid(gu.reshape(experts, width // 128, 128, 2 * f).transpose(2, 1, 0, 3)),
        "w_down": laid(np.asarray(L0_ffn_w_down).transpose(1, 0, 2)),
        "sw_gate_up": laid(sgu.reshape(width // 128, 128, -1).transpose(1, 0, 2)),
        "sw_down": laid(np.asarray(L0_ffn_sw_down).reshape(-1, 128, width).transpose(1, 0, 2)),
    }
    nc = bacc.Bacc("TRN2", target_bir_lowering=False, num_devices=1)
    args = {name: nc.dram_tensor(name, a.shape, mybir.dt.from_np(a.dtype), kind="ExternalInput").ap()
            for name, a in arrays.items()}
    tokens = xs.shape[0]
    slots = tokens * TOP + EXPERTS * P
    normed = nc.dram_tensor("normed", (tokens, width), F32, kind="Internal").ap()
    expert_out = nc.dram_tensor("expert_out", (slots, width), F32, kind="Internal").ap()
    out = nc.dram_tensor("out", (tokens, width), F32, kind="ExternalOutput").ap()
    build_xattn_moe(nc, **args, normed=normed, expert_out=expert_out, out=out)
    r = run_bass_kernel_spmd(nc, [arrays], core_ids=[0])
    return r.results[0]["out"].reshape(_OUT[0])
```
